# Optimizing a Trainium2 kernel written in Bass

```python
import numpy as np
import jax
import jax.numpy as jnp

def _softmax(x, axis=-1):
    return jax.nn.softmax(x, axis=axis)

def _gelu(x):
    return jax.nn.gelu(x, approximate=True)

def _silu(x):
    return jax.nn.silu(x)

def _sigmoid(x):
    return jax.nn.sigmoid(x)

def _layernorm(x, axis=-1, eps=1e-05):
    m = jnp.mean(x, axis=axis, keepdims=True)
    v = jnp.var(x, axis=axis, keepdims=True)
    return (x - m) / jnp.sqrt(v + eps)

def _scatter_add(tgt, idx, src, axis=0):
    return tgt.at[idx].add(src)

def _segment_sum(src, seg, n):
    return jax.ops.segment_sum(src, seg, n)
kernel_name = 'mk_vit_tower_cls_d2_tok_img1024_r4_7c70e9'

def setup_inputs(seed: int=0):
    np.random.seed(seed)
    _w = jnp.asarray

    def _rec_inputs():
        import jax
        import jax.numpy as jnp
        _rk = jax.random.key(seed)
        x = -0.00016672 + 0.999947 * jax.random.normal(jax.random.fold_in(_rk, 1), (32, 3, 96, 96), jnp.float32)
        cls_tok = 0.02 * jax.random.normal(jax.random.fold_in(_rk, 5), (1, 1, 256), jnp.float32)
        return (x, cls_tok)
    x, cls_tok = _rec_inputs()

    def _L0_tok_setup():
        import jax, jax.numpy as jnp
        import numpy as np
        IMG = 96
        PATCH = 16
        C_IN = 3
        EMBED = 256
        NPH = IMG // PATCH
        NUM_PATCHES = NPH * NPH
        PATCH_DIM = PATCH * PATCH * C_IN
        key = jax.random.key(seed)
        k_x, k_w, k_b, k_cls, k_pos = jax.random.split(key, 5)
        x = jax.random.normal(k_x, (64, C_IN, IMG, IMG), dtype=jnp.float32)
        W = jax.random.normal(k_w, (EMBED, PATCH_DIM), dtype=jnp.float32) * (1.0 / np.sqrt(PATCH_DIM))
        b = jax.random.normal(k_b, (EMBED,), dtype=jnp.float32) * 0.01
        cls_token = jax.random.normal(k_cls, (1, 1, EMBED), dtype=jnp.float32) * 0.02
        pos_embed = jax.random.normal(k_pos, (1, NUM_PATCHES + 1, EMBED), dtype=jnp.float32) * 0.02
        return {'x': x, 'W': W, 'b': b, 'cls_token': cls_token, 'pos_embed': pos_embed}
    _L0_tok_all = _L0_tok_setup()
    _L0_tok_in = {k: v for k, v in _L0_tok_all.items() if k in ('W', 'b', 'cls_token', 'pos_embed')}
    del _L0_tok_all

    def _L0_attn_setup():
        import math
        import jax, jax.numpy as jnp
        import numpy as np
        D_MODEL = 256
        N_HEADS = 16
        HEAD_DIM = D_MODEL // N_HEADS
        ROPE_THETA = 10000.0

        def _apply_rope(t, offset=0):
            B, H, T, Dh = t.shape
            inv_freq = 1.0 / ROPE_THETA ** (jnp.arange(0, Dh, 2, dtype=jnp.float32) / Dh)
            pos = jnp.arange(T, dtype=jnp.float32) + offset
            ang = pos[:, None] * inv_freq[None, :]
            cos = jnp.concatenate([jnp.cos(ang), jnp.cos(ang)], axis=-1)
            sin = jnp.concatenate([jnp.sin(ang), jnp.sin(ang)], axis=-1)
            t1, t2 = (t[..., :Dh // 2], t[..., Dh // 2:])
            rot = jnp.concatenate([-t2, t1], axis=-1)
            return t * cos + rot * sin

        def _forward(x, Wq, Wk, Wv, Wo):
            B, T, _ = x.shape
            scale = 1.0 / math.sqrt(HEAD_DIM)

            def split_heads(y):
                return y.reshape(B, T, N_HEADS, HEAD_DIM).transpose(0, 2, 1, 3)
            q = split_heads(x @ Wq.T)
            k = split_heads(x @ Wk.T)
            v = split_heads(x @ Wv.T)
            q = _apply_rope(q)
            k = _apply_rope(k)
            scores = jnp.einsum('bhtd,bhsd->bhts', q, k) * scale
            causal = jnp.triu(jnp.ones((T, T), dtype=bool), k=1)
            scores = jnp.where(causal[None, None], -jnp.inf, scores)
            attn = jax.nn.softmax(scores, axis=-1)
            attn = jnp.nan_to_num(attn, nan=0.0)
            out = jnp.einsum('bhts,bhsd->bhtd', attn, v)
            out = out.transpose(0, 2, 1, 3).reshape(B, T, N_HEADS * HEAD_DIM)
            return out @ Wo.T
        key = jax.random.key(seed)
        ks = jax.random.split(key, 5)
        B, T = (4, 512)
        w_scale = math.sqrt(2.0 / (D_MODEL + D_MODEL))
        return {'x': jax.random.normal(ks[0], (B, T, D_MODEL), dtype=jnp.float32), 'Wq': jax.random.normal(ks[1], (D_MODEL, D_MODEL), dtype=jnp.float32) * w_scale, 'Wk': jax.random.normal(ks[2], (D_MODEL, D_MODEL), dtype=jnp.float32) * w_scale, 'Wv': jax.random.normal(ks[3], (D_MODEL, D_MODEL), dtype=jnp.float32) * w_scale, 'Wo': jax.random.normal(ks[4], (D_MODEL, D_MODEL), dtype=jnp.float32) * w_scale}
    _L0_attn_all = _L0_attn_setup()
    _L0_attn_in = {k: v for k, v in _L0_attn_all.items() if k in ('Wq', 'Wk', 'Wv', 'Wo')}
    del _L0_attn_all

    def _L0_ffn_setup():
        import jax, jax.numpy as jnp
        import numpy as np
        D_MODEL = 256
        HIDDEN = 1024
        NUM_EXPERTS = 8
        TOP_K = 2
        key = jax.random.key(seed)
        k_x, k_g, k_in, k_out = jax.random.split(key, 4)
        bound_in = 1.0 / HIDDEN
        bound_out = 1.0 / D_MODEL
        x = jax.random.normal(k_x, (2, 512, D_MODEL), dtype=jnp.float32)
        w_gate = jax.random.uniform(k_g, (NUM_EXPERTS, D_MODEL), dtype=jnp.float32, minval=-D_MODEL ** (-0.5), maxval=D_MODEL ** (-0.5))
        w_in = jax.random.uniform(k_in, (NUM_EXPERTS, HIDDEN, D_MODEL), dtype=jnp.float32, minval=-bound_in, maxval=bound_in)
        w_out = jax.random.uniform(k_out, (NUM_EXPERTS, D_MODEL, HIDDEN), dtype=jnp.float32, minval=-bound_out, maxval=bound_out)
        return {'x': x, 'w_gate': w_gate, 'w_in': w_in, 'w_out': w_out}
    _L0_ffn_all = _L0_ffn_setup()
    _L0_ffn_in = {k: v for k, v in _L0_ffn_all.items() if k in ('w_gate', 'w_in', 'w_out')}
    del _L0_ffn_all

    def _L1_attn_setup():
        import jax, jax.numpy as jnp
        import numpy as np
        DIM = 256
        H = 16
        HD = DIM // H
        R = 8
        QK = 32
        B = 4
        S = 256
        EPS = 1e-05

        def _lin(x, W, b):
            return x @ W.T + b

        def _ln(x, g, b):
            m = x.mean(-1, keepdims=True)
            v = ((x - m) ** 2).mean(-1, keepdims=True)
            return (x - m) / jnp.sqrt(v + EPS) * g + b
        key = jax.random.key(seed)
        ks = iter(jax.random.split(key, 32))

        def w(shape, fan):
            s = 1.0 / np.sqrt(fan)
            return jax.random.uniform(next(ks), shape, jnp.float32, -s, s)
        d = {}
        d['x'] = jax.random.normal(next(ks), (B, S, DIM), jnp.float32)
        d['Wq'] = w((DIM, DIM), DIM)
        d['bq'] = w((DIM,), DIM)
        d['Wk'] = w((DIM, DIM), DIM)
        d['bk'] = w((DIM,), DIM)
        d['Wv'] = w((HD * R, DIM), DIM)
        d['bv'] = w((HD * R,), DIM)
        d['Wqv'] = w((QK * H, DIM), DIM)
        d['bqv'] = w((QK * H,), DIM)
        d['Ws'] = w((1, HD + QK), HD + QK)
        d['bs'] = w((1,), HD + QK)
        d['Wf'] = w((DIM, DIM), DIM)
        d['bf'] = w((DIM,), DIM)
        d['Wr1'] = w((2 * DIM, DIM), DIM)
        d['br1'] = w((2 * DIM,), DIM)
        d['Wr2'] = w((DIM, 2 * DIM), 2 * DIM)
        d['br2'] = w((DIM,), 2 * DIM)
        d['g1'] = jnp.ones((DIM,), jnp.float32)
        d['b1'] = jnp.zeros((DIM,), jnp.float32)
        d['g2'] = jnp.ones((DIM,), jnp.float32)
        d['b2'] = jnp.zeros((DIM,), jnp.float32)
        return d
    _L1_attn_all = _L1_attn_setup()
    _L1_attn_in = {k: v for k, v in _L1_attn_all.items() if k in ('Wq', 'bq', 'Wk', 'bk', 'Wv', 'bv', 'Wqv', 'bqv', 'Ws', 'bs', 'Wf', 'bf', 'Wr1', 'br1', 'Wr2', 'br2', 'g1', 'b1', 'g2', 'b2')}
    del _L1_attn_all

    def _L1_ffn_setup():
        import jax, jax.numpy as jnp
        import numpy as np
        EPS = 1e-06
        LN_EPS = 1e-05

        def _absmean_core(W):
            gamma = jnp.mean(jnp.abs(W)) + EPS
            Ws = W / gamma
            Wq = jnp.sign(Ws) * jnp.minimum(jnp.round(jnp.abs(Ws)), 1.0)
            return (Wq, gamma)

        @jax.custom_vjp
        def absmean(W):
            return _absmean_core(W)[0]

        def _absmean_fwd(W):
            Wq, gamma = _absmean_core(W)
            return (Wq, gamma)

        def _absmean_bwd(gamma, g):
            return (g / gamma,)
        absmean.defvjp(_absmean_fwd, _absmean_bwd)

        def layernorm(x, w, b, eps=LN_EPS):
            mu = jnp.mean(x, axis=-1, keepdims=True)
            var = jnp.mean((x - mu) ** 2, axis=-1, keepdims=True)
            return (x - mu) * jax.lax.rsqrt(var + eps) * w + b
        key = jax.random.key(seed)
        k1, k2, k3 = jax.random.split(key, 3)
        d, h = (256, 1024)
        B, T = (8, 512)
        return {'x': jax.random.normal(k1, (B, T, d), jnp.float32), 'W_fc': jax.random.normal(k2, (h, d), jnp.float32), 'ln_w': jnp.ones((h,), jnp.float32), 'ln_b': jnp.zeros((h,), jnp.float32), 'W_proj': jax.random.normal(k3, (d, h), jnp.float32)}
    _L1_ffn_all = _L1_ffn_setup()
    _L1_ffn_in = {k: v for k, v in _L1_ffn_all.items() if k in ('W_fc', 'ln_w', 'ln_b', 'W_proj')}
    del _L1_ffn_all
    return {'x': x, 'cls_tok': cls_tok, 'L0_tok_W': _L0_tok_in['W'], 'L0_tok_b': _L0_tok_in['b'], 'L0_tok_cls_token': _L0_tok_in['cls_token'], 'L0_tok_pos_embed': _L0_tok_in['pos_embed'], 'L0_attn_Wq': _L0_attn_in['Wq'], 'L0_attn_Wk': _L0_attn_in['Wk'], 'L0_attn_Wv': _L0_attn_in['Wv'], 'L0_attn_Wo': _L0_attn_in['Wo'], 'L0_ffn_w_gate': _L0_ffn_in['w_gate'], 'L0_ffn_w_in': _L0_ffn_in['w_in'], 'L0_ffn_w_out': _L0_ffn_in['w_out'], 'L1_attn_Wq': _L1_attn_in['Wq'], 'L1_attn_bq': _L1_attn_in['bq'], 'L1_attn_Wk': _L1_attn_in['Wk'], 'L1_attn_bk': _L1_attn_in['bk'], 'L1_attn_Wv': _L1_attn_in['Wv'], 'L1_attn_bv': _L1_attn_in['bv'], 'L1_attn_Wqv': _L1_attn_in['Wqv'], 'L1_attn_bqv': _L1_attn_in['bqv'], 'L1_attn_Ws': _L1_attn_in['Ws'], 'L1_attn_bs': _L1_attn_in['bs'], 'L1_attn_Wf': _L1_attn_in['Wf'], 'L1_attn_bf': _L1_attn_in['bf'], 'L1_attn_Wr1': _L1_attn_in['Wr1'], 'L1_attn_br1': _L1_attn_in['br1'], 'L1_attn_Wr2': _L1_attn_in['Wr2'], 'L1_attn_br2': _L1_attn_in['br2'], 'L1_attn_g1': _L1_attn_in['g1'], 'L1_attn_b1': _L1_attn_in['b1'], 'L1_attn_g2': _L1_attn_in['g2'], 'L1_attn_b2': _L1_attn_in['b2'], 'L1_ffn_W_fc': _L1_ffn_in['W_fc'], 'L1_ffn_ln_w': _L1_ffn_in['ln_w'], 'L1_ffn_ln_b': _L1_ffn_in['ln_b'], 'L1_ffn_W_proj': _L1_ffn_in['W_proj']}

def reference(x, cls_tok, L0_tok_W, L0_tok_b, L0_tok_cls_token, L0_tok_pos_embed, L0_attn_Wq, L0_attn_Wk, L0_attn_Wv, L0_attn_Wo, L0_ffn_w_gate, L0_ffn_w_in, L0_ffn_w_out, L1_attn_Wq, L1_attn_bq, L1_attn_Wk, L1_attn_bk, L1_attn_Wv, L1_attn_bv, L1_attn_Wqv, L1_attn_bqv, L1_attn_Ws, L1_attn_bs, L1_attn_Wf, L1_attn_bf, L1_attn_Wr1, L1_attn_br1, L1_attn_Wr2, L1_attn_br2, L1_attn_g1, L1_attn_b1, L1_attn_g2, L1_attn_b2, L1_ffn_W_fc, L1_ffn_ln_w, L1_ffn_ln_b, L1_ffn_W_proj):
    import jax
    import jax.numpy as jnp

    def _L0_tok_ref(x, W, b, cls_token, pos_embed):
        import jax, jax.numpy as jnp
        import numpy as np
        IMG = 96
        PATCH = 16
        C_IN = 3
        EMBED = 256
        NPH = IMG // PATCH
        NUM_PATCHES = NPH * NPH
        PATCH_DIM = PATCH * PATCH * C_IN
        B, C, H, Wd = x.shape
        nph, npw = (H // PATCH, Wd // PATCH)
        patches = x.reshape(B, C, nph, PATCH, npw, PATCH)
        patches = patches.transpose(0, 2, 4, 1, 3, 5)
        patches = patches.reshape(B, nph * npw, C * PATCH * PATCH)
        proj = jnp.einsum('bnd,ed->bne', patches, W) + b
        cls = jnp.broadcast_to(cls_token, (B, 1, cls_token.shape[-1]))
        out = jnp.concatenate([cls, proj], axis=1) + pos_embed
        return out

    def _L0_attn_ref(x, Wq, Wk, Wv, Wo):
        import math
        import jax, jax.numpy as jnp
        import numpy as np
        D_MODEL = 256
        N_HEADS = 16
        HEAD_DIM = D_MODEL // N_HEADS
        ROPE_THETA = 10000.0

        def _apply_rope(t, offset=0):
            B, H, T, Dh = t.shape
            inv_freq = 1.0 / ROPE_THETA ** (jnp.arange(0, Dh, 2, dtype=jnp.float32) / Dh)
            pos = jnp.arange(T, dtype=jnp.float32) + offset
            ang = pos[:, None] * inv_freq[None, :]
            cos = jnp.concatenate([jnp.cos(ang), jnp.cos(ang)], axis=-1)
            sin = jnp.concatenate([jnp.sin(ang), jnp.sin(ang)], axis=-1)
            t1, t2 = (t[..., :Dh // 2], t[..., Dh // 2:])
            rot = jnp.concatenate([-t2, t1], axis=-1)
            return t * cos + rot * sin

        def _forward(x, Wq, Wk, Wv, Wo):
            B, T, _ = x.shape
            scale = 1.0 / math.sqrt(HEAD_DIM)

            def split_heads(y):
                return y.reshape(B, T, N_HEADS, HEAD_DIM).transpose(0, 2, 1, 3)
            q = split_heads(x @ Wq.T)
            k = split_heads(x @ Wk.T)
            v = split_heads(x @ Wv.T)
            q = _apply_rope(q)
            k = _apply_rope(k)
            scores = jnp.einsum('bhtd,bhsd->bhts', q, k) * scale
            causal = jnp.triu(jnp.ones((T, T), dtype=bool), k=1)
            scores = jnp.where(causal[None, None], -jnp.inf, scores)
            attn = jax.nn.softmax(scores, axis=-1)
            attn = jnp.nan_to_num(attn, nan=0.0)
            out = jnp.einsum('bhts,bhsd->bhtd', attn, v)
            out = out.transpose(0, 2, 1, 3).reshape(B, T, N_HEADS * HEAD_DIM)
            return out @ Wo.T
        return _forward(x, Wq, Wk, Wv, Wo)

    def _L0_ffn_ref(x, w_gate, w_in, w_out):
        import jax, jax.numpy as jnp
        import numpy as np
        D_MODEL = 256
        HIDDEN = 1024
        NUM_EXPERTS = 8
        TOP_K = 2
        B, S, D = x.shape
        E = w_in.shape[0]
        xt = x.reshape(-1, D)
        logits = (xt @ w_gate.T).astype(jnp.float32)
        top_logits, top_idx = jax.lax.top_k(logits, TOP_K)
        top_gates = jax.nn.softmax(top_logits, axis=-1).astype(x.dtype)
        gates = (jax.nn.one_hot(top_idx, E, dtype=x.dtype) * top_gates[..., None]).sum(axis=1)
        y = jnp.zeros_like(xt)
        for e in range(E):
            h = xt @ w_in[e].T
            y = y + gates[:, e:e + 1] * (h @ w_out[e].T)
        return y.reshape(B, S, D)

    def _L1_attn_ref(x, Wq, bq, Wk, bk, Wv, bv, Wqv, bqv, Ws, bs, Wf, bf, Wr1, br1, Wr2, br2, g1, b1, g2, b2):
        import jax, jax.numpy as jnp
        import numpy as np
        DIM = 256
        H = 16
        HD = DIM // H
        R = 8
        QK = 32
        B = 4
        S = 256
        EPS = 1e-05

        def _lin(x, W, b):
            return x @ W.T + b

        def _ln(x, g, b):
            m = x.mean(-1, keepdims=True)
            v = ((x - m) ** 2).mean(-1, keepdims=True)
            return (x - m) / jnp.sqrt(v + EPS) * g + b
        b, n, _ = x.shape
        res = x
        xn = _ln(x, g1, b1)
        q = _lin(xn, Wq, bq).reshape(b, n, H, HD) / np.sqrt(HD).astype(np.float32)
        k = _lin(xn, Wk, bk).reshape(b, n, H, HD)
        score = jax.nn.softmax(jnp.einsum('bihd,bjhd->bhij', q, k), axis=-1)
        v = _lin(xn, Wv, bv).reshape(b, n, R, HD)
        out = jnp.einsum('bhij,bjrd->bihrd', score, v)
        qv = _lin(xn, Wqv, bqv).reshape(b, n, H, 1, QK) / np.sqrt(QK).astype(np.float32)
        qv = jnp.broadcast_to(qv, (b, n, H, R, QK))
        comp = jnp.concatenate([qv, out], axis=-1) @ Ws.T + bs
        comp = jax.nn.softmax(comp, axis=3)
        out = (comp * out).sum(axis=3).reshape(b, n, DIM)
        out = res + _lin(out, Wf, bf)
        res2 = out
        on = _ln(out, g2, b2)
        ffn = _lin(jax.nn.relu(_lin(on, Wr1, br1)), Wr2, br2)
        return res2 + ffn

    def _L1_ffn_ref(x, W_fc, ln_w, ln_b, W_proj):
        import jax, jax.numpy as jnp
        import numpy as np
        EPS = 1e-06
        LN_EPS = 1e-05

        def _absmean_core(W):
            gamma = jnp.mean(jnp.abs(W)) + EPS
            Ws = W / gamma
            Wq = jnp.sign(Ws) * jnp.minimum(jnp.round(jnp.abs(Ws)), 1.0)
            return (Wq, gamma)

        @jax.custom_vjp
        def absmean(W):
            return _absmean_core(W)[0]

        def _absmean_fwd(W):
            Wq, gamma = _absmean_core(W)
            return (Wq, gamma)

        def _absmean_bwd(gamma, g):
            return (g / gamma,)
        absmean.defvjp(_absmean_fwd, _absmean_bwd)

        def layernorm(x, w, b, eps=LN_EPS):
            mu = jnp.mean(x, axis=-1, keepdims=True)
            var = jnp.mean((x - mu) ** 2, axis=-1, keepdims=True)
            return (x - mu) * jax.lax.rsqrt(var + eps) * w + b
        h = jnp.einsum('btd,hd->bth', x, absmean(W_fc))
        h = jax.nn.gelu(h, approximate=False)
        h = layernorm(h, ln_w, ln_b)
        return jnp.einsum('bth,dh->btd', h, absmean(W_proj))
    h = _L0_tok_ref(x, L0_tok_W, L0_tok_b, L0_tok_cls_token, L0_tok_pos_embed)
    h = jnp.concatenate([jnp.broadcast_to(cls_tok, (h.shape[0], 1, h.shape[2])), h], axis=1)
    h = h + _L0_attn_ref(_layernorm(h, axis=-1), L0_attn_Wq, L0_attn_Wk, L0_attn_Wv, L0_attn_Wo)
    h = h + _L0_ffn_ref(_layernorm(h, axis=-1), L0_ffn_w_gate, L0_ffn_w_in, L0_ffn_w_out)
    h = h + _L1_attn_ref(_layernorm(h, axis=-1), L1_attn_Wq, L1_attn_bq, L1_attn_Wk, L1_attn_bk, L1_attn_Wv, L1_attn_bv, L1_attn_Wqv, L1_attn_bqv, L1_attn_Ws, L1_attn_bs, L1_attn_Wf, L1_attn_bf, L1_attn_Wr1, L1_attn_br1, L1_attn_Wr2, L1_attn_br2, L1_attn_g1, L1_attn_b1, L1_attn_g2, L1_attn_b2)
    h = h + _L1_ffn_ref(_layernorm(h, axis=-1), L1_ffn_W_fc, L1_ffn_ln_w, L1_ffn_ln_b, L1_ffn_W_proj)
    return h

_drawn_inputs = setup_inputs


def setup_inputs(seed=0):
    import zlib

    import numpy as np

    out = dict(_drawn_inputs(seed))
    spreads = {'L1_attn_g1': (1.0, 0.6),
     'L1_attn_b1': (0.0, 0.8),
     'L1_attn_g2': (1.0, 0.552),
     'L1_attn_b2': (0.0, 0.631),
     'L1_ffn_ln_w': (1.0, 0.2),
     'L1_ffn_ln_b': (0.0, 0.1)}
    factors = {'L0_tok_b': 3.421,
     'L0_ffn_w_gate': 8.0,
     'L0_ffn_w_in': 8.0,
     'L0_ffn_w_out': 8.0,
     'L1_attn_Wq': 8.0,
     'L1_attn_bq': 8.0,
     'L1_attn_Wk': 8.0,
     'L1_attn_bk': 8.0,
     'L1_attn_bv': 8.0,
     'L1_attn_Wqv': 8.0,
     'L1_attn_bqv': 8.0,
     'L1_attn_Ws': 8.0,
     'L1_attn_bf': 2.764,
     'L1_attn_br1': 6.867,
     'L1_attn_br2': 3.81}
    for name, (base, spread) in spreads.items():
        noise = np.random.default_rng([zlib.crc32(name.encode()), seed]).standard_normal(out[name].shape)
        drawn = base * np.exp(spread * noise) if base else spread * noise
        out[name] = jnp.asarray(drawn.astype(out[name].dtype))
    for name, factor in factors.items():
        out[name] = (out[name] * factor).astype(out[name].dtype)
    return out
```

```python
from contextlib import ExitStack

import numpy as np

import concourse.bass as bass
from concourse import mybir

F32 = mybir.dt.float32
F32R = mybir.dt.float32r
BF16 = mybir.dt.bfloat16
ALU = mybir.AluOpType
ACT = mybir.ActivationFunctionType
AX = mybir.AxisListType.X

B, IMG, PATCH, CIN = 32, 96, 16, 3
D, H, HD, E, HID = 256, 16, 16, 8, 1024
S = (IMG // PATCH) ** 2 + 2
G = 3
R = G * S
T = -(-B // G)
LAST_SKIP = (G * T - B) * S
P = 128
NP = CIN * PATCH * PATCH // P
DC = D // P
HC = HID // P
RK = 8
QK = 32
HF = H // 2
VW = RK * HD
VE = VW + RK + 1
EPS = 1e-5
LOG_ZERO = -30000.0
MASKED = -1e30
SCALE = HD ** -0.5

CI, CH, CB, CT, CC, CS, CK, CM = np.cumsum([0, P, HF, G, E * E, HD, HD, 4]).tolist()
CW = CM + HF * S
G1, B1, G2, B2, BQ, BK, BR1, LNB, BQV, WSQ = np.cumsum([0, 2, 2, 2, 2, 2, 2, 4, HC, 4]).tolist()
VC = WSQ + 1
TOK, POS, BV, BF, BR2, WSO, BS = np.cumsum([0, D, D, VW, D, D, HD]).tolist()
RW = BS + 1
A_P, A_QKV, A_O, A_END = np.cumsum([0, NP * D, DC * 3 * D, DC * D]).tolist()
W2 = VW + RK + H
C_QK, C_V, C_G, C_F, C_R1, C_R2, C_END = np.cumsum([0, DC * 2 * D, DC * W2, DC * E, DC * D, DC * 2 * D, 4 * D]).tolist()
CHUNK = C_END // E
PV_GROUPS = [(0, 3), (3, 3), (6, 3), (9, 3), (12, 2), (14, 2)]
GS = 12
MS = 11


def constants():
    c = np.zeros((P, CW), np.float32)
    c[:, CI:CI + P] = np.eye(P)
    p = np.arange(P)
    c[:, CH:CH + HF] = p[:, None] // HD == np.arange(HF)
    c[:, CB:CB + G] = np.where(p[:, None] // S == np.arange(G), 0.0, LOG_ZERO)
    c[:, CT:CT + E * E] = (np.arange(E)[None, :] < np.arange(E)[:, None]).astype(np.float32).ravel()
    inv = (np.float32(1.0) / np.float32(10000.0) ** (np.arange(0, HD, 2, dtype=np.float32) / np.float32(HD)))
    ang = (p % S).astype(np.float32)[:, None] * inv.astype(np.float32)[None, :]
    c[:, CC:CC + HD] = np.concatenate([np.cos(ang), np.cos(ang)], 1)
    c[:, CS:CS + HD] = np.concatenate([-np.sin(ang), np.sin(ang)], 1)
    c[:, CK:CK + 4] = p[:, None] // QK == np.arange(4)
    c[:, CM:] = np.tile(np.where(np.arange(S)[None, :] > (p % S)[:, None], MASKED, 0.0), (1, HF))
    return c


def stand(eng, passed):
    eng.sem_inc(passed, 1)


def since(eng, sem, value):
    if not isinstance(value, int) or value > 0:
        eng.wait_ge(sem, value)


def vit_tower(nc, x_tiles, consts, vectors, rows, w_a, w_c, wqv, w_in, w_out, fc, proj, lnw, out):
    with ExitStack() as ctx:
        def sb(name, shape, dt=F32):
            return ctx.enter_context(nc.sbuf_tensor(name, shape, dt))

        def sems(names):
            return [ctx.enter_context(nc.semaphore(n)) for n in names.split()]

        cst = sb("cst", [P, CW])
        vec = sb("vec", [P, VC])
        row = sb("row", [P, RW])
        h = sb("h", [P, T, D])
        raw = sb("raw", [P, C_END])
        wa = sb("wa", [P, 2, A_END], F32R)
        wc = sb("wc", [P, 2, C_END], F32R)
        we_h = sb("we_h", [P, DC, E, D], F32R)
        we_l = sb("we_l", [P, DC, E, D], F32R)
        ebuf = sb("ebuf", [P, 2, HC * D])
        x_raw = sb("x_raw", [P, NP * R])
        xs = sb("xs", [P, 2, NP * R], F32R)
        p_exp = sb("p_exp", [P, H, R])
        pt = sb("pt", [P, H, R])
        k_exp = sb("k_exp", [P, 2, HF, R])
        q_exp = sb("q_exp", [P, 2, G, R + S])
        sc = sb("sc", [P, H, S])
        o1 = sb("o1", [P, H, VE])
        v0 = sb("v0", [P, H, HD + 1])
        v1 = sb("v1", [P, VE])
        xth = [sb(f"xth{i}", [P, DC, R], F32R) for i in range(3)]
        xtl = [sb(f"xtl{i}", [P, DC, R], F32R) for i in range(3)]
        xn = sb("xn", [P, D])
        att = sb("att", [P, D])
        x1 = sb("x1", [P, D])
        x2 = sb("x2", [P, D])
        r2 = sb("r2", [P, D])
        x3 = sb("x3", [P, D])
        y2 = sb("y2", [P, DC, R])
        idb = sb("idb", [P, P], BF16)
        cmask = sb("cmask", [P, HF * S], BF16)
        half = sb("half", [P, 1])
        ones = sb("ones", [P, P])
        small = sb("small", [P, 6 * 20])
        smax = sb("smax", [P, H])
        rinv0 = sb("rinv0", [P, H])
        gl = sb("gl", [P, 8, E])
        g8 = sb("g8", [P, 2, E, E])
        qvs = sb("qvs", [P, H])
        cb = sb("cb", [P, H])
        vtab = sb("vtab", [P, VW + RK])
        mx = sb("mx", [P, 3, H * RK])
        mr = sb("mr", [P, 3, H])
        th = sb("th", [P, 8])
        o1f = o1[:].rearrange("p h d -> p (h d)")
        rc, rs, rq = (o1f[:, i * 2 * D:(i + 1) * 2 * D] for i in range(3))
        x1b = raw[:, 0:T * D].rearrange("p (t d) -> p t d", t=T)
        ptf = pt[:].rearrange("p h r -> p (h r)")
        r32 = x_raw[:, 0:4 * R]
        rh = xs[:, 0, 0:4 * R].rearrange("p (j r) -> p j r", j=4)
        rl = xs[:, 1, 0:4 * R].rearrange("p (j r) -> p j r", j=4)
        fct = wa[:, 0, 0:DC * HID].rearrange("p (c n) -> p c n", c=DC)
        projt = wa[:, 1, 0:HC * D].rearrange("p (c n) -> p c n", c=HC)
        gel = ebuf[:, 0, 0:HID]
        gw = ebuf[:, 1, 0:HID]
        bw = ebuf[:, 0, HID:HID + D]
        gth = we_h[:, 0].rearrange("p e d -> p (e d)")[:, 0:HC * R].rearrange("p (c r) -> p c r", c=HC)
        gtl = we_h[:, 1].rearrange("p e d -> p (e d)")[:, 0:HC * R].rearrange("p (c r) -> p c r", c=HC)
        lnwt = k_exp[:].rearrange("p f h r -> p (f h r)")[:, 0:HID]
        ident = cst[:, CI:CI + P]
        hmask = cst[:, CH:CH + HF].unsqueeze(2).broadcast_to([P, HF, R])

        bk = [ctx.enter_context(nc.psum_tensor(f"bank{i}", [P, 512], F32)) for i in range(3)]
        score = ctx.enter_context(nc.psum_tensor("score", [P, 2, 512], F32))
        tb = [ctx.enter_context(nc.psum_tensor(f"tb{i}", [P, 512], F32)) for i in range(2)]
        bz = ctx.enter_context(nc.psum_tensor("bz", [P, 512], F32))
        bk2 = lambda i: score[:, i, :]

        cst_in, vec_in, row_in, wp_in, wqkv_in, wo_in, wc_in, wqv_in, x_in, expert_in, fc_in, lnw_in, stored = sems(
            "cst_in vec_in row_in wp_in wqkv_in wo_in wc_in wqv_in x_in expert_in fc_in lnw_in stored")
        init, table, wa_hi, wa_lo, wc_split, x_split, prep, prep_mm = sems(
            "init table wa_hi wa_lo wc_split x_split prep prep_mm")
        patch_mm, embedded, qkv_mm, roped_parts, roped, v0_ready, qkT_mm = sems(
            "patch_mm embedded qkv_mm roped_parts roped v0_ready qkT_mm")
        q_ready, k_ready, s_mm, s_max, shifted, exps, pt_mm, pt_act, pt_dve = sems(
            "q_ready k_ready s_mm s_max shifted exps pt_mm pt_act pt_dve")
        pv0_mm, rinv0_ready, o_ready, wo_mm, res0 = sems("pv0_mm rinv0_ready o_ready wo_mm res0")
        combined, we_hi, we_lo = sems("combined we_hi we_lo")
        gate_mm, gate_step, gate_exp, moe_mm, moe_acc = sems("gate_mm gate_step gate_exp moe_mm moe_acc")
        q1_mm, kv1_mm, v1_ready, pv1_mm, pv1_out, mix_step, mix_exp, x1_kept = sems(
            "q1_mm kv1_mm v1_ready pv1_mm pv1_out mix_step mix_exp x1_kept")
        wf_mm, r2_ready, h_r2, wr1_mm, relu_hi, relu_32, relu_lo, wr2_mm, res1 = sems(
            "wf_mm r2_ready h_r2 wr1_mm relu_hi relu_32 relu_lo wr2_mm res1")
        tern, tern_mm, fc_mm, gelu, g_stat, g_rstd, gw_ready, gT_mm, gT_hi, gT_lo, bw_ready = sems(
            "tern tern_mm fc_mm gelu g_stat g_rstd gw_ready gT_mm gT_hi gT_lo bw_ready")
        proj_mm, hb_ready, done = sems("proj_mm hb_ready done")

        def norm_place(name, at):
            stat, rstd, normed = sems(f"{name}_stat {name}_rstd {name}_normed")
            return dict(stat=stat, rstd=rstd, normed=normed, at=small[:, at * 20:(at + 1) * 20])

        def turn_place(name):
            mm, hi, lo = sems(f"{name}_mm {name}_hi {name}_lo")
            return dict(mm=mm, hi=hi, lo=lo)

        nA, n1, n2, n3, n4 = (norm_place(f"norm{i}", i) for i in range(5))
        nD = norm_place("normD", 5)
        tA, tO, t1, t2, t3, t4, tD = (turn_place(n) for n in ("xT", "oT", "c1T", "c2T", "attT", "c3T", "dT"))
        aff2, aff4 = sems("aff2 aff4")
        dve_passed, gp_passed = sems("dve_passed gp_passed")

        block = ctx.enter_context(nc.Block())

        @block.sync
        def _(sp):
            sp.dma_start(x_raw[:], x_tiles[0]).then_inc(x_in, 16)
            sp.dma_start(raw[:, A_P:A_QKV], w_a[:, A_P:A_QKV]).then_inc(wp_in, 16)
            sp.dma_start(row[:], rows).then_inc(row_in, 16)
            sp.dma_start(cst[:], consts).then_inc(cst_in, 16)
            sp.dma_start(raw[:, A_QKV:A_O], w_a[:, A_QKV:A_O]).then_inc(wqkv_in, 16)
            sp.dma_start(raw[:, A_O:A_END], w_a[:, A_O:A_END]).then_inc(wo_in, 16)
            sp.dma_start(vec[:], vectors).then_inc(vec_in, 16)
            sp.dma_start(ptf[:, 0:4 * D], wqv).then_inc(wqv_in, 16)

            def load_expert(e):
                sp.dma_start(ebuf[:, 0, :], w_in[e]).then_inc(expert_in, 16)
                sp.dma_start(ebuf[:, 1, :], w_out[e]).then_inc(expert_in, 16)

            def load_x(t):
                sp.wait_ge(x_split, 2 * t)
                sp.dma_start(x_raw[:], x_tiles[t]).then_inc(x_in, 16)

            load_expert(0)
            sp.wait_ge(wa_hi, 3)
            sp.wait_ge(wa_lo, 3)
            sp.dma_start(raw[:], w_c).then_inc(wc_in, 16)
            load_x(1)
            with sp.Fori(1, E) as t:
                load_x(t + 1)
                sp.wait_ge(combined, t)
                load_expert(t)
            load_x(E + 1)
            load_x(E + 2)
            sp.wait_ge(combined, E)
            sp.dma_start(ebuf[:, 0, :], fc).then_inc(fc_in, 16)
            sp.dma_start(ebuf[:, 1, :], proj).then_inc(fc_in, 16)
            sp.wait_ge(s_mm, 2 * T)
            sp.dma_start(lnwt[0:R], lnw).then_inc(lnw_in, 16)
            with sp.Fori(0, T - 1) as t:
                sp.wait_ge(done, t + 1)
                sp.dma_start(out[bass.ds(t * R, R), :], h[0:R, t, :]).then_inc(stored, 16)
            sp.wait_ge(done, T)
            sp.dma_start(out[B * S - (R - LAST_SKIP):B * S, :], h[LAST_SKIP:R, T - 1, :]).then_inc(stored, 16)
            sp.wait_ge(stored, 16 * T)

        @block.gpsimd
        def _(gp):
            gp.memset(half[:], -0.5).then_inc(init, 1)
            gp.memset(ones[:], 1.0).then_inc(init, 1)
            gp.memset(q_exp[:], 0.0).then_inc(init, 1)
            gp.memset(v0[:], 1.0).then_inc(init, 1)
            gp.memset(v1[:], 1.0).then_inc(init, 1)

            def split_x(t):
                gp.wait_ge(x_in, 16 * (t + 1))
                since(gp, patch_mm, t)
                stand(gp, gp_passed)
                gp.tensor_copy(xs[:, 0, :], x_raw[:]).then_inc(x_split, 1)
                gp.wait_ge(x_split, 2 * t + 1)
                gp.tensor_tensor(xs[:, 1, :], x_raw[:], xs[:, 0, :].bitcast(F32), ALU.subtract).then_inc(x_split, 1)

            def rstd(n, t, sem=None):
                gp.wait_ge(n["stat"], 3 * t + 3)
                gp.tensor_tensor(n["at"][0:R, 9:10], n["at"][0:R, 8:9], half[0:R], ALU.pow).then_inc(n["rstd"], 1)

            def a_step(t, split=True):
                rstd(nA, t)
                if split:
                    split_x(t + 1)
                gp.wait_ge(roped_parts, 3 * t + 3)
                since(gp, qkT_mm, t)
                gp.tensor_tensor(rq[0:R], rc[0:R], rs[0:R], ALU.add).then_inc(roped, 1)

            split_x(0)
            a_step(0)
            gp.wait_ge(wc_in, 16)
            gp.wait_ge(prep, 5)
            def a_step_wc(t):
                a_step(t)
                part = bass.ds((t - 1) * CHUNK, CHUNK)
                gp.tensor_copy(wc[:, 0, part], raw[:, part]).then_inc(wc_split, 1)
                gp.wait_ge(wc_split, 2 * t - 1)
                gp.tensor_tensor(wc[:, 1, part], raw[:, part], wc[:, 0, part].bitcast(F32), ALU.subtract).then_inc(wc_split, 1)

            a_step_wc(1)
            with gp.Fori(2, E + 1) as t:
                a_step_wc(t)
            a_step(E + 1)
            a_step(E + 2, False)

            def c1(t):
                rstd(n1, t)

            def c2(t):
                rstd(n2, t)
                gp.wait_ge(n2["normed"], t + 1)
                gp.tensor_tensor(x1b[0:R, t, :], x1[0:R], row[0:R, BF:BF + D], ALU.add).then_inc(x1_kept, 1)
                rstd(n3, t)

            def c3(t):
                rstd(n4, t)
                gp.wait_ge(n4["normed"], t + 1)
                gp.tensor_tensor(r2[0:R], r2[0:R], row[0:R, BR2:BR2 + D], ALU.add).then_inc(h_r2, 1)
                gp.wait_ge(h_r2, 2 * t + 1)
                gp.tensor_tensor(h[0:R, t, :], h[0:R, t, :], r2[0:R], ALU.add).then_inc(h_r2, 1)

            c1(0)
            c2(0)
            c1(1)
            c2(1)
            c1(2)
            c3(0)
            with gp.Fori(3, T) as t:
                c2(t - 1)
                c1(t)
                c3(t - 2)
            c2(T - 1)
            c3(T - 2)
            c3(T - 1)

            def d2(t):
                gp.wait_ge(g_stat, 4 * t + 4)
                gp.tensor_tensor(th[0:R, 7:8], th[0:R, 6:7], half[0:R], ALU.pow).then_inc(g_rstd, 1)
                gp.wait_ge(nD["normed"], t + 1)
                gp.tensor_tensor(h[0:R, t, :], h[0:R, t, :], bw[0:R], ALU.add).then_inc(hb_ready, 1)

            rstd(nD, 0)
            gp.wait_ge(bw_ready, 1)
            rstd(nD, 1)
            d2(0)
            with gp.Fori(2, T) as t:
                rstd(nD, t)
                d2(t - 1)
            d2(T - 1)

        @block.scalar
        def _(act):
            for i, (a, b, s) in enumerate(((A_P, A_QKV, wp_in), (A_QKV, A_O, wqkv_in), (A_O, A_END, wo_in))):
                act.wait_ge(s, 16)
                act.activation(wa[:, 0, a:b], raw[:, a:b], ACT.Copy).then_inc(wa_hi, 1)

            def turn_hi(tp, xh, src, t, free=None):
                act.wait_ge(tp["mm"], t + 1)
                if free:
                    since(act, *free)
                act.activation(xh[:], src, ACT.Copy).then_inc(tp["hi"], 1)

            def two(x):
                return x.rearrange("p (c r) -> p c r", c=DC)

            def affine_hi(tp, aff, xh, t, free):
                act.wait_ge(aff, 2 * t + 2)
                since(act, *free)
                act.activation(xh[:], y2[:], ACT.Copy).then_inc(tp["hi"], 1)

            def a1_x(t):
                turn_hi(tA, xth[0], two(bk[0][:, 256:256 + 2 * R]), t, (qkv_mm, t))

            def a1_v(t):
                act.wait_ge(qkv_mm, t + 1)
                since(act, pv0_mm, t)
                act.activation(v0[0:R, :, 0:HD], bk[2][0:R, 0:D].rearrange("p (h d) -> p h d", h=H),
                               ACT.Copy).then_inc(v0_ready, 1)

            def a1_q(t):
                act.wait_ge(qkT_mm, t + 1)
                since(act, s_mm, t)
                for f in range(2):
                    act.activation(qd(f),
                                   bk[2][:, f * R:(f + 1) * R].rearrange("p (b s) -> p b s", b=G),
                                   ACT.Copy).then_inc(q_ready, 1)

            def qd(f):
                return q_exp[:, f, :, 0:S]

            def softmax_exp(n):
                act.wait_ge(shifted, 2 * n + 2)
                since(act, pt_mm, 4 * n)
                for b in range(G):
                    act.activation(p_exp[0:R, :, b * S:(b + 1) * S], sc[0:R], ACT.Exp,
                                   bias=cst[0:R, CB + b:CB + b + 1], scale=SCALE).then_inc(exps, 1)

            def pt_out(n, free):
                for g in (0, 2):
                    act.wait_ge(pt_mm, 4 * n + g + 1)
                    if g == 0:
                        since(act, *free)
                    act.activation(pt[0:R, 4 * g:4 * g + 4, :], tb[0][0:R, 0:4 * R].rearrange("p (h r) -> p h r", h=4),
                                   ACT.Copy).then_inc(pt_act, 1)

            def a2_o(t):
                turn_hi(tO, xth[1], two(bk2(1)[:, 0:2 * R]), t, (wo_mm, t))

            def expert_hi(e):
                act.wait_ge(combined, e + 1)
                act.activation(we_h[:, :, e, :], bz[:].rearrange("p (m n) -> p m n", m=DC), ACT.Copy).then_inc(we_hi, 1)

            act.wait_ge(init, 5)
            act.wait_ge(cst_in, 16)
            act.wait_ge(vec_in, 16)
            a1_x(0)
            a1_v(0)
            a1_q(0)

            def a_step(t, expert):
                softmax_exp(t - 1)
                pt_out(t - 1, (pv0_mm, t - 1))
                a1_x(t)
                a1_v(t)
                a2_o(t - 1)
                if expert:
                    expert_hi(t - 1)
                a1_q(t)

            a_step(1, True)
            with act.Fori(2, E + 1) as t:
                a_step(t, True)
            a_step(E + 1, False)
            a_step(E + 2, False)
            softmax_exp(T - 1)
            pt_out(T - 1, (pv0_mm, T - 1))
            a2_o(T - 1)

            def c1_x(t):
                turn_hi(t1, xth[0], two(bk[0][:, 0:2 * R]), t, (moe_mm, 4 * t))

            def c1_gate(t):
                act.wait_ge(gate_step, GS * t + 3)
                act.activation(gl[0:R, 3, :], gl[0:R, 2, :], ACT.Exp).then_inc(gate_exp, 1)

            def c2_x(t):
                affine_hi(t2, aff2, xth[1], t, (kv1_mm, t))

            def c2_q(t):
                act.wait_ge(q1_mm, t + 1)
                for f in range(2):
                    act.activation(qd(f), tb[0][:, f * R:(f + 1) * R].rearrange("p (b s) -> p b s", b=G),
                                   ACT.Identity, bias=vec[:, BQ + f:BQ + f + 1]).then_inc(q_ready, 1)

            def c2_pt(t):
                if isinstance(t, int) and t == 0:
                    pt_out(T, (pv0_mm, T))
                else:
                    pt_out(t + T, (pv1_mm, 6 * t))

            def c2_pv(t):
                for g, (h0, k) in enumerate(PV_GROUPS):
                    act.wait_ge(pv1_mm, 6 * t + g + 1)
                    if g == 0:
                        since(act, mix_step, MS * t)
                    act.activation(o1[0:R, h0:h0 + k, :],
                                   score[0:R, g % 2, 0:k * VE].rearrange("p (h d) -> p h d", h=k), ACT.Copy).then_inc(pv1_out, 1)

            def c2_mix(t):
                act.wait_ge(mix_step, MS * t + 5)
                act.activation(mx[0:R, 1, :], mx[0:R, 0, :], ACT.Exp).then_inc(mix_exp, 1)

            def c3_att(t):
                turn_hi(t3, xth[2], two(bz[:, 0:2 * R]), t, (wr1_mm, t))

            def c3_x(t):
                affine_hi(t4, aff4, xth[2], t, (wf_mm, t + 1))

            def c3_relu(t):
                act.wait_ge(relu_32, 4 * t + 4)
                since(act, wr2_mm, t)
                act.activation(rh[:], r32.rearrange("p (j r) -> p j r", j=4), ACT.Copy).then_inc(relu_hi, 1)

            def c_step(t, one, two_, three):
                if two_:
                    c2_x(t - 1)
                if one:
                    c1_x(t)
                if three:
                    c3_att(t - 2)
                if two_:
                    c2_q(t - 1)
                if one:
                    c1_gate(t)
                if two_:
                    softmax_exp(t - 1 + T)
                if three:
                    c3_x(t - 2)
                if two_:
                    c2_pt(t - 1)
                if three:
                    c3_relu(t - 2)
                if two_:
                    c2_pv(t - 1)
                    c2_mix(t - 1)

            c_step(0, True, False, False)
            c_step(1, True, True, False)
            c_step(2, True, True, True)
            with act.Fori(3, T) as t:
                c_step(t, True, True, True)
            c_step(T, False, True, True)
            c_step(T + 1, False, False, True)

            def d1(t):
                turn_hi(tD, xth[0], two(bk[0][:, 0:2 * R]), t, (fc_mm, 2 * t))

            def d1_gelu(t):
                for q in range(2):
                    act.wait_ge(fc_mm, 2 * t + q + 1)
                    if q == 0:
                        since(act, gw_ready, t)
                    act.activation(gel[0:R, q * 512:(q + 1) * 512], bk[1 + q][0:R, :], ACT.Gelu).then_inc(gelu, 1)

            def d2_hi(t):
                for q in range(2):
                    act.wait_ge(gT_mm, 2 * t + q + 1)
                    if q == 0:
                        since(act, proj_mm, t)
                    act.activation(gth[:, 4 * q:4 * q + 4, :], score[:, q, 0:4 * R].rearrange("p (c r) -> p c r", c=4),
                                   ACT.Copy).then_inc(gT_hi, 1)

            d1(0)
            d1_gelu(0)
            d1(1)
            d2_hi(0)
            d1_gelu(1)
            with act.Fori(2, T) as t:
                d1(t)
                d2_hi(t - 1)
                d1_gelu(t)
            d2_hi(T - 1)

        @block.vector
        def _(dve):
            V = nc.vector

            def norm(n, src, dst, t, free=None):
                a = n["at"][0:R]
                stand(dve, dve_passed)
                V.bn_stats(a[:, 0:6], src).then_inc(n["stat"], 1)
                dve.wait_ge(n["stat"], 3 * t + 1)
                stand(dve, dve_passed)
                V.bn_aggr(a[:, 6:8], a[:, 0:6]).then_inc(n["stat"], 1)
                dve.wait_ge(n["stat"], 3 * t + 2)
                V.tensor_scalar(a[:, 8:9], a[:, 7:8], EPS, None, ALU.add).then_inc(n["stat"], 1)
                dve.wait_ge(n["rstd"], t + 1)
                if free:
                    since(dve, *free)
                V.tensor_scalar(dst, src, a[:, 6:7], a[:, 9:10], ALU.subtract, ALU.mult).then_inc(n["normed"], 1)

            def two(x):
                return x.rearrange("p (c r) -> p c r", c=DC)

            def turn_lo(tp, xh, xl, src, t):
                dve.wait_ge(tp["hi"], t + 1)
                V.tensor_tensor(xl[:], src, xh[:].bitcast(F32), ALU.subtract).then_inc(tp["lo"], 1)

            def affine_lo(tp, aff, xh, xl, src, g, b, t):
                dve.wait_ge(tp["mm"], t + 1)
                since(dve, tp["lo"], t)
                for c in range(DC):
                    V.tensor_scalar(y2[:, c, :], src[:, c, :], vec[:, g + c:g + c + 1], vec[:, b + c:b + c + 1],
                                    ALU.mult, ALU.add).then_inc(aff, 1)
                dve.wait_ge(aff, 2 * t + 2)
                dve.wait_ge(tp["hi"], t + 1)
                V.tensor_tensor(xl[:], y2[:], xh[:].bitcast(F32), ALU.subtract).then_inc(tp["lo"], 1)

            dve.wait_ge(init, 5)
            dve.wait_ge(row_in, 16)
            V.tensor_tensor(row[0:R, TOK:TOK + D], row[0:R, TOK:TOK + D], row[0:R, POS:POS + D], ALU.add).then_inc(table, 1)
            for i, (a, b) in enumerate(((A_P, A_QKV), (A_QKV, A_O), (A_O, A_END))):
                dve.wait_ge(wa_hi, i + 1)
                V.tensor_tensor(wa[:, 1, a:b], raw[:, a:b], wa[:, 0, a:b].bitcast(F32), ALU.subtract).then_inc(wa_lo, 1)
            dve.wait_ge(cst_in, 16)
            V.tensor_copy(idb[:], ident).then_inc(table, 1)
            V.tensor_copy(cmask[:], cst[:, CM:CW]).then_inc(table, 1)

            def a1_embed(t):
                dve.wait_ge(patch_mm, t + 1)
                V.tensor_tensor(h[0:R, t, :], bk[0][0:R, 0:D], row[0:R, TOK:TOK + D], ALU.add).then_inc(embedded, 1)
                dve.wait_ge(embedded, t + 1)
                norm(nA, h[0:R, t, :], xn[0:R], t, (tA["mm"], t))

            def a1_x(t):
                turn_lo(tA, xth[0], xtl[0], two(bk[0][:, 256:256 + 2 * R]), t)

            def a1_rope(t):
                dve.wait_ge(qkv_mm, t + 1)
                since(dve, roped, t)
                qk = bk[1][0:R, :].rearrange("p (h d) -> p h d", d=HD)
                cos = cst[0:R, CC:CC + HD].unsqueeze(1).broadcast_to([R, 2 * H, HD])
                V.tensor_tensor(rc[0:R].rearrange("p (h d) -> p h d", d=HD), qk, cos, ALU.mult).then_inc(roped_parts, 1)
                for i in range(2):
                    a, b = i * HD // 2, (1 - i) * HD // 2
                    sin = cst[0:R, CS + a:CS + a + HD // 2].unsqueeze(1).broadcast_to([R, 2 * H, HD // 2])
                    V.tensor_tensor(rs[0:R].rearrange("p (h d) -> p h d", d=HD)[:, :, a:a + HD // 2],
                                    qk[:, :, b:b + HD // 2], sin, ALU.mult).then_inc(roped_parts, 1)

            def a1_k(t):
                dve.wait_ge(qkT_mm, t + 1)
                since(dve, s_mm, t)
                for f in range(2):
                    kT = bk[1][:, f * R:(1 + f) * R].unsqueeze(1).broadcast_to([P, HF, R])
                    V.tensor_tensor(k_exp[:, f], kT, hmask, ALU.mult).then_inc(k_ready, 1)

            def softmax_shift(n):
                dve.wait_ge(s_mm, n + 1)
                s = score[0:R, :, 0:HF * S].rearrange("p f (h j) -> p f h j", j=S)
                V.tensor_reduce(smax[0:R].rearrange("p (f h) -> p f h", f=2), s, AX, ALU.max).then_inc(s_max, 1)
                dve.wait_ge(s_max, n + 1)
                since(dve, exps, 3 * n)
                for f in range(2):
                    V.tensor_tensor(sc[0:R, f * HF:(f + 1) * HF, :], s[:, f],
                                    smax[0:R, f * HF:(f + 1) * HF].unsqueeze(2).broadcast_to([R, HF, S]),
                                    ALU.subtract).then_inc(shifted, 1)

            def pt_out(n, free):
                for g in (1, 3):
                    dve.wait_ge(pt_mm, 4 * n + g + 1)
                    if g == 1:
                        since(dve, *free)
                    V.tensor_copy(pt[0:R, 4 * g:4 * g + 4, :],
                                  tb[1][0:R, 0:4 * R].rearrange("p (h r) -> p h r", h=4)).then_inc(pt_dve, 1)

            def a2_o(t):
                dve.wait_ge(pv0_mm, t + 1)
                o = score[0:R, 0, 0:H * (HD + 1)].rearrange("p (h d) -> p h d", h=H)
                V.reciprocal(rinv0[0:R], o[:, :, HD]).then_inc(rinv0_ready, 1)
                dve.wait_ge(rinv0_ready, t + 1)
                since(dve, tO["mm"], t)
                V.tensor_tensor(att[0:R].rearrange("p (h d) -> p h d", h=H), o[:, :, 0:HD],
                                rinv0[0:R].unsqueeze(2).broadcast_to([R, H, HD]), ALU.mult).then_inc(o_ready, 1)

            def a2_lo(t):
                turn_lo(tO, xth[1], xtl[1], two(bk2(1)[:, 0:2 * R]), t)

            def a2_res(t):
                dve.wait_ge(wo_mm, t + 1)
                V.tensor_tensor(h[0:R, t, :], bk2(1)[0:R, 256:512], h[0:R, t, :], ALU.add).then_inc(res0, 1)

            def expert_lo(e):
                dve.wait_ge(we_hi, e + 1)
                V.tensor_tensor(we_l[:, :, e, :], bz[:].rearrange("p (m n) -> p m n", m=DC),
                                we_h[:, :, e, :].bitcast(F32), ALU.subtract).then_inc(we_lo, 1)

            a1_embed(0)
            a1_x(0)
            a1_rope(0)
            a1_k(0)

            dve.wait_ge(wc_in, 16)
            dve.wait_ge(vec_in, 16)
            wv = raw[:, C_V:C_G].rearrange("p (c n) -> p c n", c=DC)
            tmp = p_exp[:].rearrange("p h r -> p (h r)")
            wso = row[:, WSO:WSO + HD].unsqueeze(1)
            for c in range(DC):
                V.tensor_tensor(tmp[:, c * VW:(c + 1) * VW].rearrange("p (r d) -> p r d", r=RK),
                                wv[:, c, 0:VW].rearrange("p (r d) -> p r d", r=RK), wso.broadcast_to([P, RK, HD]),
                                ALU.mult).then_inc(table, 1)
            V.tensor_tensor(tmp[:, 2 * VW:3 * VW].rearrange("p (r d) -> p r d", r=RK),
                            row[:, BV:BV + VW].rearrange("p (r d) -> p r d", r=RK), wso.broadcast_to([P, RK, HD]),
                            ALU.mult).then_inc(table, 1)
            dve.wait_ge(table, 6)
            V.tensor_reduce(wv[:, :, VW:VW + RK], tmp[:, 0:2 * VW].rearrange("p (c r d) -> p c r d", c=DC, r=RK),
                            AX, ALU.add).then_inc(prep, 1)
            V.tensor_reduce(vtab[:, VW:VW + RK], tmp[:, 2 * VW:3 * VW].rearrange("p (r d) -> p r d", r=RK),
                            AX, ALU.add).then_inc(prep, 1)
            V.tensor_copy(vtab[:, 0:VW], row[:, BV:BV + VW]).then_inc(prep, 1)
            bl = tmp[:, 3 * VW:3 * VW + 4]
            V.tensor_scalar(bl, cst[:, CK:CK + 4], vec[:, WSQ:WSQ + 1], float(QK) ** -0.5, ALU.mult, ALU.mult).then_inc(table, 1)
            dve.wait_ge(table, 7)
            for c in range(4):
                V.tensor_scalar(tmp[:, 3 * VW + 4 + 4 * c:3 * VW + 8 + 4 * c], bl, vec[:, BQV + c:BQV + c + 1], None,
                                ALU.mult).then_inc(table, 1)
            dve.wait_ge(prep_mm, 1)
            V.tensor_copy(wv[:, :, VW + RK:W2], bz[:, 0:2 * H].rearrange("p (c h) -> p c h", c=DC)).then_inc(prep, 1)
            V.tensor_scalar(cb[:], bz[:, 2 * H:3 * H], row[:, BS:BS + 1], None, ALU.add).then_inc(prep, 1)

            def a_step(t, expert):
                softmax_shift(t - 1)
                a1_embed(t)
                pt_out(t - 1, (pv0_mm, t - 1))
                a1_x(t)
                a2_o(t - 1)
                a1_rope(t)
                a2_lo(t - 1)
                if expert:
                    expert_lo(t - 1)
                a2_res(t - 1)
                a1_k(t)

            a_step(1, True)
            with dve.Fori(2, E + 1) as t:
                a_step(t, True)
            a_step(E + 1, False)
            a_step(E + 2, False)
            softmax_shift(T - 1)
            pt_out(T - 1, (pv0_mm, T - 1))
            a2_o(T - 1)
            a2_lo(T - 1)
            a2_res(T - 1)

            def c1_norm(t):
                dve.wait_ge(res0, t + 1)
                norm(n1, h[0:R, t, :], xn[0:R], t, (t1["mm"], t) if not isinstance(t, int) or t else (tA["mm"], T))

            def c1_x(t):
                turn_lo(t1, xth[0], xtl[0], two(bk[0][:, 0:2 * R]), t)

            def c1_gates(t):
                k = [GS * t]

                def step(ins):
                    k[0] = k[0] + 1
                    ins.then_inc(gate_step, 1)
                    dve.wait_ge(gate_step, k[0])

                g = gl[0:R]
                dve.wait_ge(gate_mm, t + 1)
                step(V.tensor_copy(g[:, 0, :], bk[0][0:R, 256:256 + E]))
                step(V.tensor_reduce(g[:, 1, 0:1], g[:, 0, :], AX, ALU.max))
                step(V.tensor_scalar(g[:, 2, :], g[:, 0, :], g[:, 1, 0:1], None, ALU.subtract))
                mine = g[:, 0, :].unsqueeze(2).broadcast_to([R, E, E])
                other = g[:, 0, :].unsqueeze(1).broadcast_to([R, E, E])
                before = cst[0:R, CT:CT + E * E].rearrange("p (a b) -> p a b", a=E)
                step(V.tensor_tensor(g8[0:R, 0], other, mine, ALU.is_gt))
                step(V.tensor_tensor(g8[0:R, 1], other, mine, ALU.is_equal))
                step(V.tensor_tensor(g8[0:R, 1], g8[0:R, 1], before, ALU.mult))
                step(V.tensor_tensor(g8[0:R, 0], g8[0:R, 0], g8[0:R, 1], ALU.add))
                step(V.tensor_reduce(g[:, 4, :], g8[0:R, 0], AX, ALU.add))
                dve.wait_ge(gate_exp, t + 1)
                step(V.scalar_tensor_tensor(g[:, 5, :], g[:, 4, :], 1.5, g[:, 3, :], ALU.is_lt, ALU.mult))
                step(V.tensor_reduce(g[:, 6, 0:1], g[:, 5, :], AX, ALU.add))
                step(V.reciprocal(g[:, 6, 1:2], g[:, 6, 0:1]))
                step(V.tensor_scalar(g[:, 7, :], g[:, 5, :], g[:, 6, 1:2], None, ALU.mult))

            def c1_acc(t, pairs):
                for p in pairs:
                    dve.wait_ge(moe_mm, 4 * t + p + 1)
                    for i in range(2):
                        e = 2 * p + i
                        since(dve, moe_acc, 8 * t + e)
                        V.scalar_tensor_tensor(h[0:R, t, :], bk[1 + p % 2][0:R, i * D:(i + 1) * D],
                                               gl[0:R, 7, e:e + 1], h[0:R, t, :], ALU.mult, ALU.add).then_inc(moe_acc, 1)

            def c2_norms(t):
                dve.wait_ge(moe_acc, 8 * t + 8)
                since(dve, x1_kept, t)
                norm(n2, h[0:R, t, :], x1[0:R], t)
                dve.wait_ge(n2["normed"], t + 1)
                norm(n3, x1[0:R], x2[0:R], t, (t2["mm"], t))

            def c2_x(t):
                affine_lo(t2, aff2, xth[1], xtl[1], two(tb[0][:, 0:2 * R]), G1, B1, t)

            def c2_k(t):
                dve.wait_ge(kv1_mm, t + 1)
                for f in range(2):
                    kT = tb[1][:, f * R:(1 + f) * R].unsqueeze(1).broadcast_to([P, HF, R])
                    V.scalar_tensor_tensor(k_exp[:, f], kT, vec[:, BK + f:BK + f + 1], hmask,
                                           ALU.add, ALU.mult).then_inc(k_ready, 1)

            def c2_v(t):
                since(dve, pv1_mm, 6 * t)
                since(dve, mix_step, MS * t)
                V.tensor_tensor(v1[0:R, 0:VE - 1], tb[1][0:R, 2 * R:2 * R + VE - 1], vtab[0:R], ALU.add).then_inc(v1_ready, 1)
                V.tensor_tensor(qvs[0:R], tb[1][0:R, 2 * R + VE - 1:2 * R + W2], cb[0:R], ALU.add).then_inc(v1_ready, 1)

            def c2_pt(t):
                if isinstance(t, int) and t == 0:
                    pt_out(T, (pv0_mm, T))
                else:
                    pt_out(t + T, (pv1_mm, 6 * t))

            def c2_mix(t):
                k = [MS * t]

                def step(ins):
                    k[0] = k[0] + 1
                    ins.then_inc(mix_step, 1)
                    dve.wait_ge(mix_step, k[0])

                def over(x):
                    return x.unsqueeze(2).broadcast_to([R, H, RK])

                c = mx[0:R, 0].rearrange("p (h r) -> p h r", h=H)
                ex = mx[0:R, 1].rearrange("p (h r) -> p h r", h=H)
                w = mx[0:R, 2].rearrange("p (h r) -> p h r", h=H)
                m = [mr[0:R, i] for i in range(3)]
                dve.wait_ge(pv1_out, 6 * t + 6)
                step(V.reciprocal(m[0], o1[0:R, :, VE - 1]))
                step(V.tensor_tensor(c, o1[0:R, :, VW:VW + RK], over(m[0]), ALU.mult))
                step(V.tensor_tensor(c, c, over(qvs[0:R]), ALU.add))
                step(V.tensor_reduce(m[1], c, AX, ALU.max))
                step(V.tensor_tensor(c, c, over(m[1]), ALU.subtract))
                dve.wait_ge(mix_exp, t + 1)
                step(V.tensor_reduce(m[1], ex, AX, ALU.add))
                step(V.reciprocal(m[2], m[1]))
                step(V.tensor_tensor(m[2], m[2], m[0], ALU.mult))
                step(V.tensor_tensor(w, ex, over(m[2]), ALU.mult))
                o = o1[0:R, :, 0:VW].rearrange("p h (r d) -> p h r d", r=RK)
                step(V.tensor_tensor(o, o, w.unsqueeze(3).broadcast_to([R, H, RK, HD]), ALU.mult))
                since(dve, t3["mm"], t)
                if isinstance(t, int) and t == 0:
                    dve.wait_ge(tO["mm"], T)
                step(V.tensor_reduce(att[0:R].rearrange("p (h d) -> p h d", h=H), o.rearrange("p h r d -> p h d r"), AX, ALU.add))

            def c3_att(t):
                turn_lo(t3, xth[2], xtl[2], two(bz[:, 0:2 * R]), t)

            def c3_r2(t):
                dve.wait_ge(wf_mm, t + 1)
                dve.wait_ge(x1_kept, t + 1)
                since(dve, h_r2, 2 * t)
                V.tensor_tensor(r2[0:R], bz[0:R, 256:512], x1b[0:R, t, :], ALU.add).then_inc(r2_ready, 1)
                dve.wait_ge(r2_ready, t + 1)
                norm(n4, r2[0:R], x3[0:R], t, (t4["mm"], t))

            def c3_x(t):
                affine_lo(t4, aff4, xth[2], xtl[2], two(bz[:, 0:2 * R]), G2, B2, t)

            def c3_relu(t):
                dve.wait_ge(wr1_mm, t + 1)
                for j in range(4):
                    V.tensor_scalar(r32[:, j * R:(j + 1) * R], bz[:, j * R:(j + 1) * R], vec[:, BR1 + j:BR1 + j + 1], 0.0,
                                    ALU.add, ALU.max).then_inc(relu_32, 1)
                dve.wait_ge(relu_32, 4 * t + 4)
                dve.wait_ge(relu_hi, t + 1)
                V.tensor_tensor(rl[:], r32.rearrange("p (j r) -> p j r", j=4), rh[:].bitcast(F32), ALU.subtract).then_inc(relu_lo, 1)

            def c3_res(t):
                dve.wait_ge(wr2_mm, t + 1)
                dve.wait_ge(h_r2, 2 * t + 2)
                V.tensor_tensor(h[0:R, t, :], bz[0:R, 0:D], h[0:R, t, :], ALU.add).then_inc(res1, 1)

            def c_step(t, one, two_, three):
                if two_:
                    c2_norms(t - 1)
                if one:
                    c1_norm(t)
                if two_:
                    c2_x(t - 1)
                if one:
                    c1_x(t)
                if three:
                    c3_att(t - 2)
                if two_:
                    c2_k(t - 1)
                    c2_v(t - 1)
                if one:
                    c1_gates(t)
                if two_:
                    softmax_shift(t - 1 + T)
                if three:
                    c3_r2(t - 2)
                if one:
                    c1_acc(t, (0, 1))
                if three:
                    c3_x(t - 2)
                if two_:
                    c2_pt(t - 1)
                if three:
                    c3_relu(t - 2)
                if one:
                    c1_acc(t, (2, 3))
                if three:
                    c3_res(t - 2)
                if two_:
                    c2_mix(t - 1)

            c_step(0, True, False, False)

            dve.wait_ge(fc_in, 32)
            for i in range(2):
                V.tensor_reduce(th[:, i:i + 1], ebuf[:, i, :], AX, ALU.add, apply_absolute_value=True).then_inc(tern, 1)
            dve.wait_ge(tern_mm, 1)
            V.tensor_scalar(th[:, 2:4], tb[0][:, 0:2], 0.5 / (D * HID), 0.5e-6, ALU.mult, ALU.add).then_inc(tern, 1)
            dve.wait_ge(tern, 3)
            V.tensor_scalar(th[:, 4:6], th[:, 2:4], -1.0, None, ALU.mult).then_inc(tern, 1)
            dve.wait_ge(tern, 4)
            dve.wait_ge(wo_mm, T)
            for i in range(2):
                V.tensor_scalar(wa[:, i, 0:HC * D], ebuf[:, i, :], th[:, 4 + i:5 + i], None, ALU.is_lt).then_inc(tern, 1)
            dve.wait_ge(tern, 6)
            for i in range(2):
                V.scalar_tensor_tensor(wa[:, i, 0:HC * D], ebuf[:, i, :], th[:, 2 + i:3 + i],
                                       wa[:, i, 0:HC * D].bitcast(F32), ALU.is_gt, ALU.subtract).then_inc(tern, 1)

            c_step(1, True, True, False)
            c_step(2, True, True, True)
            with dve.Fori(3, T) as t:
                c_step(t, True, True, True)
            c_step(T, False, True, True)
            c_step(T + 1, False, False, True)

            def d1_norm(t):
                dve.wait_ge(res1, t + 1)
                norm(nD, h[0:R, t, :], xn[0:R], t, (tD["mm"], t) if not isinstance(t, int) or t else (t1["mm"], T))

            def d1_x(t):
                turn_lo(tD, xth[0], xtl[0], two(bk[0][:, 0:2 * R]), t)

            def d2_norm(t):
                st = mx[0:R, 0, 0:12]
                for q in range(2):
                    dve.wait_ge(gelu, 2 * t + q + 1)
                    V.bn_stats(st[:, 6 * q:6 * q + 6], gel[0:R, q * 512:(q + 1) * 512]).then_inc(g_stat, 1)
                dve.wait_ge(g_stat, 4 * t + 2)
                stand(dve, dve_passed)
                V.bn_aggr(mr[0:R, 0, 0:2], st).then_inc(g_stat, 1)
                dve.wait_ge(g_stat, 4 * t + 3)
                since(dve, done, t)
                V.tensor_scalar(th[0:R, 6:7], mr[0:R, 0, 1:2], EPS, None, ALU.add).then_inc(g_stat, 1)
                since(dve, gT_mm, 2 * t)
                V.scalar_tensor_tensor(gw[0:R], gel[0:R], mr[0:R, 0, 0:1], lnwt[0:R], ALU.subtract, ALU.mult).then_inc(gw_ready, 1)

            def d2_lo(t):
                for q in range(2):
                    dve.wait_ge(gT_hi, 2 * t + q + 1)
                    V.tensor_tensor(gtl[:, 4 * q:4 * q + 4, :], score[:, q, 0:4 * R].rearrange("p (c r) -> p c r", c=4),
                                    gth[:, 4 * q:4 * q + 4, :].bitcast(F32), ALU.subtract).then_inc(gT_lo, 1)

            def d2_out(t):
                dve.wait_ge(proj_mm, t + 1)
                dve.wait_ge(hb_ready, t + 1)
                dve.wait_ge(g_rstd, t + 1)
                V.scalar_tensor_tensor(h[0:R, t, :], tb[0][0:R, 0:D], th[0:R, 7:8], h[0:R, t, :],
                                       ALU.mult, ALU.add).then_inc(done, 1)

            dve.wait_ge(pv1_mm, 6 * T)
            V.tensor_copy(pt[:, 0:HC, :], vec[:, LNB:LNB + HC].unsqueeze(2).broadcast_to([P, HC, R])).then_inc(tern, 1)
            dve.wait_ge(tern_mm, 2)
            V.tensor_copy(bw[0:R], tb[1][0:R, 0:D]).then_inc(bw_ready, 1)
            d1_norm(0)
            d1_x(0)
            dve.wait_ge(lnw_in, 16)
            d1_norm(1)
            d2_norm(0)
            d1_x(1)
            d2_lo(0)
            d2_out(0)
            with dve.Fori(2, T) as t:
                d1_norm(t)
                d2_norm(t - 1)
                d1_x(t)
                d2_lo(t - 1)
                d2_out(t - 1)
            d2_norm(T - 1)
            d2_lo(T - 1)
            d2_out(T - 1)

        @block.tensor
        def _(pe):
            def mm3(dst, lh, ll, rh_, rl_, first, last):
                pe.matmul(dst, lh, rh_, start=first, stop=False)
                pe.matmul(dst, lh, rl_, start=False, stop=False)
                return pe.matmul(dst, ll, rh_, start=False, stop=last)

            def product(dst, xh, xl, w, at, width, cols):
                a, b = cols
                for c in range(DC):
                    o = at + c * width
                    last = mm3(dst, xh[:, c, :], xl[:, c, :], w[:, 0, o + a:o + b], w[:, 1, o + a:o + b], c == 0, c == DC - 1)
                return last

            def turned(dst, x):
                for c in range(DC):
                    last = pe.transpose(dst[:, c * R:(c + 1) * R], x[0:R, c * P:(c + 1) * P], cst[0:R, CI:CI + R])
                return last

            def turn(tp, dst, x, ready, t):
                pe.wait_ge(ready, t + 1)
                turned(dst, x).then_inc(tp["mm"], 1)

            def a1_patch(t):
                pe.wait_ge(x_split, 2 * t + 2)
                since(pe, tA["lo"], t)
                for c in range(NP):
                    last = mm3(bk[0][0:R, 0:D], xs[:, 0, c * R:(c + 1) * R], xs[:, 1, c * R:(c + 1) * R],
                               wa[:, 0, A_P + c * D:A_P + (c + 1) * D], wa[:, 1, A_P + c * D:A_P + (c + 1) * D],
                               c == 0, c == NP - 1)
                last.then_inc(patch_mm, 1)

            def a1_x(t):
                turn(tA, bk[0][:, 256:256 + 2 * R], xn, nA["normed"], t)

            def a1_qkv(t):
                pe.wait_ge(tA["lo"], t + 1)
                since(pe, k_ready, 2 * t)
                since(pe, q_ready, 2 * t)
                product(bk[1][0:R, :], xth[0], xtl[0], wa, A_QKV, 3 * D, (0, 2 * D))
                product(bk[2][0:R, 0:D], xth[0], xtl[0], wa, A_QKV, 3 * D, (2 * D, 3 * D)).then_inc(qkv_mm, 1)

            def a1_qkT(t):
                pe.wait_ge(roped, t + 1)
                pe.wait_ge(v0_ready, t + 1)
                turned(bk[2][:, 0:2 * R], rq[:, 0:D])
                turned(bk[1][:, 0:2 * R], rq[:, D:2 * D]).then_inc(qkT_mm, 1)

            def scores(n, causal):
                pe.wait_ge(q_ready, 2 * n + 2)
                pe.wait_ge(k_ready, 2 * n + 2)
                for f in range(2):
                    dst = score[0:R, f, 0:HF * S]
                    if causal:
                        pe.matmul(dst, idb[0:R, 0:R], cmask[0:R], start=True, stop=False)
                    for b in range(G):
                        last = pe.matmul(dst, q_exp[:, f].rearrange("p b x -> p (b x)")[:, b * R:(b + 1) * R],
                                         k_exp[:, f, :, b * S:(b + 1) * S], start=(not causal and b == 0), stop=(b == G - 1))
                last.then_inc(s_mm, 1)

            def turn_p(n):
                pe.wait_ge(exps, 3 * n + 3)
                for g in range(4):
                    if g % 2 == 0:
                        since(pe, pt_act, 2 * n + g // 2)
                    else:
                        since(pe, pt_dve, 2 * n + g // 2)
                    for i in range(4):
                        last = pe.transpose(tb[g % 2][0:R, i * R:(i + 1) * R], p_exp[0:R, 4 * g + i, :], cst[0:R, CI:CI + R])
                    last.then_inc(pt_mm, 1)

            def a2_pv(t):
                pe.wait_ge(pt_act, 2 * t + 2)
                pe.wait_ge(pt_dve, 2 * t + 2)
                pe.wait_ge(v0_ready, t + 1)
                for i in range(H):
                    last = pe.matmul(score[0:R, 0, i * (HD + 1):(i + 1) * (HD + 1)], pt[0:R, i, :], v0[0:R, i, :],
                                     start=True, stop=True)
                last.then_inc(pv0_mm, 1)

            def a2_o(t):
                turn(tO, bk2(1)[:, 0:2 * R], att, o_ready, t)

            def a2_wo(t):
                pe.wait_ge(tO["lo"], t + 1)
                product(bk2(1)[0:R, 256:512], xth[1], xtl[1], wa, A_O, D, (0, D)).then_inc(wo_mm, 1)

            def combine(e, m):
                if m == 0:
                    pe.wait_ge(expert_in, 32 * e + 32)
                    since(pe, we_lo, e)
                for c in range(HC):
                    last = pe.matmul(bz[:, m * D:(m + 1) * D], ebuf[:, 0, c * D + m * P:c * D + (m + 1) * P],
                                     ebuf[:, 1, c * D:(c + 1) * D], start=(c == 0), stop=(c == HC - 1))
                if m == DC - 1:
                    last.then_inc(combined, 1)

            pe.wait_ge(wa_lo, 3)
            pe.wait_ge(cst_in, 16)
            pe.wait_ge(table, 3)
            pe.wait_ge(init, 5)
            a1_patch(0)
            a1_x(0)
            a1_qkv(0)
            a1_qkT(0)
            pe.wait_ge(wqv_in, 16)
            pe.wait_ge(table, 11)
            tmp = p_exp[:].rearrange("p h r -> p (h r)")
            for c in range(4):
                for m in range(DC):
                    pe.matmul(bz[:, m * H + 4 * c:m * H + 4 * c + 4], ptf[:, c * D + m * P:c * D + (m + 1) * P],
                              tmp[:, 3 * VW:3 * VW + 4], start=True, stop=True)
                last = pe.matmul(bz[:, 2 * H + 4 * c:2 * H + 4 * c + 4], ones[:],
                                 tmp[:, 3 * VW + 4 + 4 * c:3 * VW + 8 + 4 * c], start=True, stop=True)
            last.then_inc(prep_mm, 1)
            pe.wait_ge(prep, 5)

            def a_step(t, expert):
                scores(t - 1, True)
                a1_patch(t)
                if expert:
                    combine(t - 1, 0)
                turn_p(t - 1)
                a1_x(t)
                a2_pv(t - 1)
                a1_qkv(t)
                a2_o(t - 1)
                if expert:
                    combine(t - 1, 1)
                a2_wo(t - 1)
                a1_qkT(t)

            a_step(1, True)
            with pe.Fori(2, E + 1) as t:
                a_step(t, True)
            a_step(E + 1, False)
            a_step(E + 2, False)
            scores(T - 1, True)
            turn_p(T - 1)
            a2_pv(T - 1)
            a2_o(T - 1)
            a2_wo(T - 1)

            def c1_x(t):
                turn(t1, bk[0][:, 0:2 * R], xn, n1["normed"], t)

            def c1_gate(t):
                pe.wait_ge(t1["lo"], t + 1)
                product(bk[0][0:R, 256:256 + E], xth[0], xtl[0], wc, C_G, E, (0, E)).then_inc(gate_mm, 1)

            def c1_moe(t, pairs):
                for p in pairs:
                    if p >= 2:
                        pe.wait_ge(moe_acc, 8 * t + 2 * (p - 1))
                    for c in range(DC):
                        last = mm3(bk[1 + p % 2][0:R, :], xth[0][:, c, :], xtl[0][:, c, :],
                                   we_h[:, c, 2 * p:2 * p + 2, :].rearrange("p e d -> p (e d)"),
                                   we_l[:, c, 2 * p:2 * p + 2, :].rearrange("p e d -> p (e d)"), c == 0, c == DC - 1)
                    last.then_inc(moe_mm, 1)

            def c2_x(t):
                since(pe, pt_act, 2 * (t + T))
                since(pe, pt_dve, 2 * (t + T))
                turn(t2, tb[0][:, 0:2 * R], x2, n3["normed"], t)

            def c2_qkv(t):
                pe.wait_ge(t2["lo"], t + 1)
                for j in range(4):
                    for c in range(DC):
                        o = C_QK + c * 2 * D + j * P
                        last = mm3(tb[j // 2][:, j % 2 * R:(j % 2 + 1) * R], wc[:, 0, o:o + P], wc[:, 1, o:o + P],
                                   xth[1][:, c, :], xtl[1][:, c, :], c == 0, c == DC - 1)
                    if j == 1:
                        last.then_inc(q1_mm, 1)
                product(tb[1][0:R, 2 * R:2 * R + W2], xth[1], xtl[1], wc, C_V, W2, (0, W2)).then_inc(kv1_mm, 1)

            def c2_pv(t):
                pe.wait_ge(pt_act, 2 * (t + T) + 2)
                pe.wait_ge(pt_dve, 2 * (t + T) + 2)
                pe.wait_ge(v1_ready, 2 * t + 2)
                for g, (h0, k) in enumerate(PV_GROUPS):
                    if g >= 2:
                        pe.wait_ge(pv1_out, 6 * t + g - 1)
                    for i in range(k):
                        last = pe.matmul(score[0:R, g % 2, i * VE:(i + 1) * VE], pt[0:R, h0 + i, :], v1[0:R, :],
                                         start=True, stop=True)
                    last.then_inc(pv1_mm, 1)

            def c3_att(t):
                since(pe, res1, t)
                pe.wait_ge(mix_step, MS * t + MS)
                turned(bz[:, 0:2 * R], att).then_inc(t3["mm"], 1)

            def c3_wf(t):
                pe.wait_ge(t3["lo"], t + 1)
                product(bz[0:R, 256:512], xth[2], xtl[2], wc, C_F, D, (0, D)).then_inc(wf_mm, 1)

            def c3_x(t):
                turn(t4, bz[:, 0:2 * R], x3, n4["normed"], t)

            def c3_r1(t):
                pe.wait_ge(t4["lo"], t + 1)
                for j in range(4):
                    for c in range(DC):
                        o = C_R1 + c * 2 * D + j * P
                        last = mm3(bz[:, j * R:(j + 1) * R], wc[:, 0, o:o + P], wc[:, 1, o:o + P],
                                   xth[2][:, c, :], xtl[2][:, c, :], c == 0, c == DC - 1)
                last.then_inc(wr1_mm, 1)

            def c3_r2(t):
                pe.wait_ge(relu_lo, t + 1)
                for j in range(4):
                    o = C_R2 + j * D
                    last = mm3(bz[0:R, 0:D], rh[:, j, :], rl[:, j, :], wc[:, 0, o:o + D], wc[:, 1, o:o + D], j == 0, j == 3)
                last.then_inc(wr2_mm, 1)

            def c_step(t, one, two_, three):
                if two_:
                    c2_x(t - 1)
                if one:
                    c1_x(t)
                if three:
                    c3_att(t - 2)
                if two_:
                    c2_qkv(t - 1)
                if one:
                    c1_gate(t)
                if three:
                    c3_wf(t - 2)
                if one:
                    c1_moe(t, (0,))
                if two_:
                    scores(t - 1 + T, False)
                if one:
                    c1_moe(t, (1,))
                if three:
                    c3_x(t - 2)
                if three:
                    c3_r1(t - 2)
                if two_:
                    turn_p(t - 1 + T)
                if one:
                    c1_moe(t, (2, 3))
                if three:
                    c3_r2(t - 2)
                if two_:
                    c2_pv(t - 1)

            pe.wait_ge(wc_split, 2 * E)
            c_step(0, True, False, False)
            pe.wait_ge(tern, 2)
            pe.wait_ge(pt_act, 2 * T)
            pe.matmul(tb[0][:, 0:2], ones[:], th[:, 0:2], start=True, stop=True).then_inc(tern_mm, 1)
            pe.wait_ge(tern, 3)
            c_step(1, True, True, False)
            c_step(2, True, True, True)
            with pe.Fori(3, T) as t:
                c_step(t, True, True, True)
            c_step(T, False, True, True)
            c_step(T + 1, False, False, True)

            pe.wait_ge(tern, 9)
            for c in range(HC):
                last = pe.matmul(tb[1][0:R, 0:D], pt[:, c, :], projt[:, c, :].bitcast(F32), start=(c == 0), stop=(c == HC - 1))
            last.then_inc(tern_mm, 1)

            def d1_x(t):
                turn(tD, bk[0][:, 0:2 * R], xn, nD["normed"], t)

            def d1_fc(t):
                pe.wait_ge(tD["lo"], t + 1)
                since(pe, gelu, 2 * t)
                for q in range(2):
                    for c in range(DC):
                        w = fct[:, c, q * 512:(q + 1) * 512]
                        pe.matmul(bk[1 + q][0:R, :], xth[0][:, c, :], w, start=(c == 0), stop=False)
                        last = pe.matmul(bk[1 + q][0:R, :], xtl[0][:, c, :], w, start=False, stop=(c == DC - 1))
                    last.then_inc(fc_mm, 1)

            def d2_turn(t):
                pe.wait_ge(gw_ready, t + 1)
                since(pe, gT_lo, 2 * t)
                for q in range(2):
                    for c in range(4):
                        k = 4 * q + c
                        last = pe.transpose(score[:, q, c * R:(c + 1) * R], gw[0:R, k * P:(k + 1) * P], cst[0:R, CI:CI + R])
                    last.then_inc(gT_mm, 1)

            def d2_proj(t):
                pe.wait_ge(gT_lo, 2 * t + 2)
                since(pe, done, t)
                for c in range(HC):
                    pe.matmul(tb[0][0:R, 0:D], gth[:, c, :], projt[:, c, :], start=(c == 0), stop=False)
                    last = pe.matmul(tb[0][0:R, 0:D], gtl[:, c, :], projt[:, c, :], start=False, stop=(c == HC - 1))
                last.then_inc(proj_mm, 1)

            d1_x(0)
            d1_fc(0)
            d1_x(1)
            d2_turn(0)
            d1_fc(1)
            d2_proj(0)
            with pe.Fori(2, T) as t:
                d1_x(t)
                d2_turn(t - 1)
                d1_fc(t)
                d2_proj(t - 1)
            d2_turn(T - 1)
            d2_proj(T - 1)


def lay_out(i):
    f = np.float32
    a = {k: np.asarray(v) for k, v in i.items()}
    n = IMG // PATCH

    def chunks(w, c):
        return w.reshape(c, P, -1).transpose(1, 0, 2).reshape(P, -1)

    def column(v, c):
        return v.reshape(c, P).T

    x = a["x"].reshape(B, CIN, n, PATCH, n, PATCH).transpose(1, 3, 5, 0, 2, 4).reshape(NP, P, B, n * n)
    xt = np.zeros((T, P, NP, G, S), f)
    for t in range(T):
        b0 = min(G * t, B - G)
        xt[t, :, :, :, 2:] = x[:, :, b0:b0 + G].transpose(1, 0, 2, 3)
    rows = np.zeros((P, RW), f)
    tok = np.concatenate([a["cls_tok"].reshape(1, D), a["L0_tok_cls_token"].reshape(1, D),
                          np.broadcast_to(a["L0_tok_b"], (S - 2, D))], 0)
    pos = np.concatenate([np.zeros((1, D), f), a["L0_tok_pos_embed"].reshape(S - 1, D)], 0)
    rows[:R, TOK:TOK + D] = np.tile(tok, (G, 1))
    rows[:R, POS:POS + D] = np.tile(pos, (G, 1))
    ws = a["L1_attn_Ws"].reshape(-1)
    for at, v in ((BV, a["L1_attn_bv"]), (BF, a["L1_attn_bf"]), (BR2, a["L1_attn_br2"]), (WSO, ws[QK:]), (BS, a["L1_attn_bs"])):
        rows[:, at:at + v.size] = v
    vectors = np.concatenate(
        [column(a["L1_attn_g1"], 2), column(a["L1_attn_b1"], 2), column(a["L1_attn_g2"], 2), column(a["L1_attn_b2"], 2),
         column(a["L1_attn_bq"], 2), column(a["L1_attn_bk"], 2), column(a["L1_attn_br1"], 4), column(a["L1_ffn_ln_b"], HC),
         column(a["L1_attn_bqv"], 4), np.tile(ws[:QK], 4)[:, None]], 1)
    w_a = np.concatenate(
        [chunks(a["L0_tok_W"].T, NP), chunks(np.concatenate([a["L0_attn_Wq"].T, a["L0_attn_Wk"].T, a["L0_attn_Wv"].T], 1), DC),
         chunks(a["L0_attn_Wo"].T, DC)], 1)
    wv = np.concatenate([a["L1_attn_Wv"].T, np.zeros((D, W2 - VW), f)], 1)
    w_c = np.concatenate(
        [chunks(np.concatenate([a["L1_attn_Wq"].T, a["L1_attn_Wk"].T], 1), DC), chunks(wv, DC), chunks(a["L0_ffn_w_gate"].T, DC),
         chunks(a["L1_attn_Wf"].T, DC), chunks(a["L1_attn_Wr1"].T, DC), chunks(a["L1_attn_Wr2"].T, 4)], 1)
    return {
        "x_tiles": xt.reshape(T, P, NP * R), "consts": constants(), "vectors": vectors, "rows": rows,
        "w_a": w_a, "w_c": w_c, "wqv": chunks(a["L1_attn_Wqv"], 4),
        "w_in": a["L0_ffn_w_in"].reshape(E, P, HC * D), "w_out": a["L0_ffn_w_out"].transpose(0, 2, 1).reshape(E, P, HC * D),
        "fc": chunks(a["L1_ffn_W_fc"].T, DC), "proj": chunks(a["L1_ffn_W_proj"].T, HC),
        "lnw": np.broadcast_to(a["L1_ffn_ln_w"], (R, HID)),
    }


def kernel(**inputs):
    import concourse.bacc as bacc
    from concourse.bass_utils import run_bass_kernel_spmd as run

    nc = bacc.Bacc("TRN2", target_bir_lowering=False, num_devices=1)
    arrays = {f"in_{k}": np.ascontiguousarray(v) for k, v in lay_out(inputs).items()}
    args = [nc.dram_tensor(k, v.shape, mybir.dt.from_np(v.dtype), kind="ExternalInput").ap() for k, v in arrays.items()]
    out = nc.dram_tensor("out_0", (B * S, D), F32, kind="ExternalOutput").ap()
    vit_tower(nc, *args, out)
    r = run(nc, [arrays], core_ids=[0])
    return r.results[0]["out_0"].reshape(B, S, D)
```

```python
from contextlib import ExitStack

import numpy as np

import concourse.bass as bass
from concourse import mybir

F32 = mybir.dt.float32
F32R = mybir.dt.float32r
BF16 = mybir.dt.bfloat16
ALU = mybir.AluOpType
ACT = mybir.ActivationFunctionType
AX = mybir.AxisListType.X

B, IMG, PATCH, CIN = 32, 96, 16, 3
D, H, HD, E, HID = 256, 16, 16, 8, 1024
S = (IMG // PATCH) ** 2 + 2
G = 3
R = G * S
T = -(-B // G)
LAST_SKIP = (G * T - B) * S
P = 128
NP = CIN * PATCH * PATCH // P
DC = D // P
HC = HID // P
RK = 8
QK = 32
HF = H // 2
VW = RK * HD
VE = VW + RK + 1
EPS = 1e-5
LOG_ZERO = -30000.0
MASKED = -1e30
SCALE = HD ** -0.5

CI, CH, CB, CT, CC, CS, CK, CM = np.cumsum([0, P, HF, G, E * E, HD, HD, 4]).tolist()
CW = CM + HF * S
G1, B1, G2, B2, BQ, BK, BR1, LNB, BQV, WSQ = np.cumsum([0, 2, 2, 2, 2, 2, 2, 4, HC, 4]).tolist()
VC = WSQ + 1
TOK, POS, BV, BF, BR2, WSO, BS = np.cumsum([0, D, D, VW, D, D, HD]).tolist()
RW = BS + 1
A_P, A_QKV, A_O, A_END = np.cumsum([0, NP * D, DC * 3 * D, DC * D]).tolist()
W2 = VW + RK + H
C_QK, C_V, C_G, C_F, C_R1, C_R2, C_END = np.cumsum([0, DC * 2 * D, DC * W2, DC * E, DC * D, DC * 2 * D, 4 * D]).tolist()
CHUNK = C_END // E
PV_GROUPS = [(0, 3), (3, 3), (6, 3), (9, 3), (12, 2), (14, 2)]
GS = 12
MS = 11


def constants():
    c = np.zeros((P, CW), np.float32)
    c[:, CI:CI + P] = np.eye(P)
    p = np.arange(P)
    c[:, CH:CH + HF] = p[:, None] // HD == np.arange(HF)
    c[:, CB:CB + G] = np.where(p[:, None] // S == np.arange(G), 0.0, LOG_ZERO)
    c[:, CT:CT + E * E] = (np.arange(E)[None, :] < np.arange(E)[:, None]).astype(np.float32).ravel()
    inv = (np.float32(1.0) / np.float32(10000.0) ** (np.arange(0, HD, 2, dtype=np.float32) / np.float32(HD)))
    ang = (p % S).astype(np.float32)[:, None] * inv.astype(np.float32)[None, :]
    c[:, CC:CC + HD] = np.concatenate([np.cos(ang), np.cos(ang)], 1)
    c[:, CS:CS + HD] = np.concatenate([-np.sin(ang), np.sin(ang)], 1)
    c[:, CK:CK + 4] = p[:, None] // QK == np.arange(4)
    c[:, CM:] = np.tile(np.where(np.arange(S)[None, :] > (p % S)[:, None], MASKED, 0.0), (1, HF))
    return c


def stand(eng, passed):
    eng.sem_inc(passed, 1)


def since(eng, sem, value):
    if not isinstance(value, int) or value > 0:
        eng.wait_ge(sem, value)


def vit_tower(nc, x_tiles, consts, vectors, rows, w_a, w_c, wqv, w_in, w_out, fc, proj, lnw, out):
    with ExitStack() as ctx:
        def sb(name, shape, dt=F32):
            return ctx.enter_context(nc.sbuf_tensor(name, shape, dt))

        def sems(names):
            return [ctx.enter_context(nc.semaphore(n)) for n in names.split()]

        cst = sb("cst", [P, CW])
        vec = sb("vec", [P, VC])
        row = sb("row", [P, RW])
        h = sb("h", [P, T, D])
        raw = sb("raw", [P, C_END])
        wa = sb("wa", [P, 2, A_END], F32R)
        wc = sb("wc", [P, 2, C_END], F32R)
        we_h = sb("we_h", [P, DC, E, D], F32R)
        we_l = sb("we_l", [P, DC, E, D], F32R)
        ebuf = sb("ebuf", [P, 2, HC * D])
        x_raw = sb("x_raw", [P, NP * R])
        xs = sb("xs", [P, 2, NP * R], F32R)
        p_exp = sb("p_exp", [P, H, R])
        pt = sb("pt", [P, H, R])
        k_exp = sb("k_exp", [P, 2, HF, R])
        q_exp = sb("q_exp", [P, 2, G, R + S])
        sc = sb("sc", [P, H, S])
        o1 = sb("o1", [P, H, VE])
        v0 = sb("v0", [P, H, HD + 1])
        v1 = sb("v1", [P, VE])
        v1_next = sb("v1_next", [P, VE - 1])
        xth = [sb(f"xth{i}", [P, DC, R], F32R) for i in range(3)]
        xtl = [sb(f"xtl{i}", [P, DC, R], F32R) for i in range(3)]
        xn = sb("xn", [P, D])
        att = sb("att", [P, D])
        x1 = sb("x1", [P, D])
        x2 = sb("x2", [P, D])
        r2 = sb("r2", [P, D])
        x3 = sb("x3", [P, D])
        y2 = sb("y2", [P, DC, R])
        scaled = sb("scaled", [P, 4, D])
        idb = sb("idb", [P, P], BF16)
        cmask = sb("cmask", [P, HF * S], BF16)
        half = sb("half", [P, 1])
        ones = sb("ones", [P, P])
        small = sb("small", [P, 6 * 20])
        smax = sb("smax", [P, H])
        rinv0 = sb("rinv0", [P, H])
        gl = sb("gl", [P, 8, E])
        g8 = sb("g8", [P, 2, E, E])
        qvs = sb("qvs", [P, T, H])
        cb = sb("cb", [P, H])
        vtab = sb("vtab", [P, VW + RK])
        mx = sb("mx", [P, 3, H * RK])
        mr = sb("mr", [P, 3, H])
        th = sb("th", [P, 6])
        grs = sb("grs", [P, T, 2])
        o1f = o1[:].rearrange("p h d -> p (h d)")
        rc, rs, rq = (o1f[:, i * 2 * D:(i + 1) * 2 * D] for i in range(3))
        x1b = raw[:, 0:T * D].rearrange("p (t d) -> p t d", t=T)
        qk_rows = raw[:, T * D:(T + 2) * D]
        r_rows = raw[:, (T + 2) * D:(T + 4) * D]
        ptf = pt[:].rearrange("p h r -> p (h r)")
        r32 = x_raw[:, 0:4 * R]
        y4 = x_raw[:, 4 * R:6 * R].rearrange("p (c r) -> p c r", c=DC)
        rh = xs[:, 0, 0:4 * R].rearrange("p (j r) -> p j r", j=4)
        rl = xs[:, 1, 0:4 * R].rearrange("p (j r) -> p j r", j=4)
        fct = wa[:, 0, 0:DC * HID].rearrange("p (c n) -> p c n", c=DC)
        projt = wa[:, 1, 0:HC * D].rearrange("p (c n) -> p c n", c=HC)
        gel = ebuf[:, 0, 0:HID]
        gw = ebuf[:, 1, 0:HID]
        bw = ebuf[:, 0, HID:HID + D]
        gth = we_h[:, 0].rearrange("p e d -> p (e d)")[:, 0:HC * R].rearrange("p (c r) -> p c r", c=HC)
        gtl = we_h[:, 1].rearrange("p e d -> p (e d)")[:, 0:HC * R].rearrange("p (c r) -> p c r", c=HC)
        lnwt = k_exp[:].rearrange("p f h r -> p (f h r)")[:, 0:HID]
        ident = cst[:, CI:CI + P]
        hmask = cst[:, CH:CH + HF].unsqueeze(2).broadcast_to([P, HF, R])

        bk = [ctx.enter_context(nc.psum_tensor(f"bank{i}", [P, 512], F32)) for i in range(3)]
        score = ctx.enter_context(nc.psum_tensor("score", [P, 2, 512], F32))
        tb = [ctx.enter_context(nc.psum_tensor(f"tb{i}", [P, 512], F32)) for i in range(2)]
        bz = ctx.enter_context(nc.psum_tensor("bz", [P, 512], F32))
        bk2 = lambda i: score[:, i, :]

        cst_in, vec_in, row_in, wp_in, wqkv_in, wo_in, wc_in, wqv_in, x_in, expert_in, fc_in, lnw_in, stored = sems(
            "cst_in vec_in row_in wp_in wqkv_in wo_in wc_in wqv_in x_in expert_in fc_in lnw_in stored")
        init, table, wa_hi, wa_lo, wc_split, x_split, prep, prep_mm = sems(
            "init table wa_hi wa_lo wc_split x_split prep prep_mm")
        patch_mm, embedded, qkv_mm, roped_parts, roped, v0_ready, qkT_mm = sems(
            "patch_mm embedded qkv_mm roped_parts roped v0_ready qkT_mm")
        q_ready, k_ready, s_mm, s_max, shifted, exps, pt_mm, pt_even, pt_odd = sems(
            "q_ready k_ready s_mm s_max shifted exps pt_mm pt_even pt_odd")
        pv0_mm, rinv0_ready, o_ready, wo_mm, res0 = sems("pv0_mm rinv0_ready o_ready wo_mm res0")
        combined, we_hi, we_lo = sems("combined we_hi we_lo")
        gate_mm, gate_step, gate_exp, moe_mm, moe_scaled, moe_acc = sems(
            "gate_mm gate_step gate_exp moe_mm moe_scaled moe_acc")
        qk1_mm, v1_mm, qk1_out, qkT1_mm, v1_ready, v1_moved, pv1_mm, pv1_out, mix_step, mix_exp, x1_kept = sems(
            "qk1_mm v1_mm qk1_out qkT1_mm v1_ready v1_moved pv1_mm pv1_out mix_step mix_exp x1_kept")
        wf_mm, r2_ready, h_r2, wr1_mm, wr1_out, r1T_mm, relu_hi, relu_32, relu_lo, wr2_mm, res1 = sems(
            "wf_mm r2_ready h_r2 wr1_mm wr1_out r1T_mm relu_hi relu_32 relu_lo wr2_mm res1")
        tern, tern_mm, fc_mm, gelu, g_stat, g_rstd, gw_ready, gT_mm, gT_hi, gT_lo, bw_ready = sems(
            "tern tern_mm fc_mm gelu g_stat g_rstd gw_ready gT_mm gT_hi gT_lo bw_ready")
        proj_mm, hb_ready, done = sems("proj_mm hb_ready done")

        def norm_place(name, at):
            stat, rstd, normed = sems(f"{name}_stat {name}_rstd {name}_normed")
            return dict(stat=stat, rstd=rstd, normed=normed, at=small[:, at * 20:(at + 1) * 20])

        def turn_place(name):
            mm, hi, lo = sems(f"{name}_mm {name}_hi {name}_lo")
            return dict(mm=mm, hi=hi, lo=lo)

        nA, n1, n2, n3, n4 = (norm_place(f"norm{i}", i) for i in range(5))
        nD = norm_place("normD", 5)
        tA, tO, t1, t2, t3, t4, tD = (turn_place(n) for n in ("xT", "oT", "c1T", "c2T", "attT", "c3T", "dT"))
        aff2, aff4 = sems("aff2 aff4")
        dve_passed, gp_passed = sems("dve_passed gp_passed")

        block = ctx.enter_context(nc.Block())

        @block.sync
        def _(sp):
            sp.dma_start(x_raw[:], x_tiles[0]).then_inc(x_in, 16)
            sp.dma_start(raw[:, A_P:A_QKV], w_a[:, A_P:A_QKV]).then_inc(wp_in, 16)
            sp.dma_start(row[:], rows).then_inc(row_in, 16)
            sp.dma_start(cst[:], consts).then_inc(cst_in, 16)
            sp.dma_start(raw[:, A_QKV:A_O], w_a[:, A_QKV:A_O]).then_inc(wqkv_in, 16)
            sp.dma_start(raw[:, A_O:A_END], w_a[:, A_O:A_END]).then_inc(wo_in, 16)
            sp.dma_start(vec[:], vectors).then_inc(vec_in, 16)
            sp.dma_start(ptf[:, 0:4 * D], wqv).then_inc(wqv_in, 16)

            def load_expert(e):
                sp.dma_start(ebuf[:, 0, :], w_in[e]).then_inc(expert_in, 16)
                sp.dma_start(ebuf[:, 1, :], w_out[e]).then_inc(expert_in, 16)

            def load_x(t):
                sp.wait_ge(x_split, 2 * t)
                sp.dma_start(x_raw[:], x_tiles[t]).then_inc(x_in, 16)

            load_expert(0)
            sp.wait_ge(wa_hi, 3)
            sp.wait_ge(wa_lo, 3)
            sp.dma_start(raw[:], w_c).then_inc(wc_in, 16)
            load_x(1)
            with sp.Fori(1, E) as t:
                load_x(t + 1)
                sp.wait_ge(combined, t)
                load_expert(t)
            load_x(E + 1)
            load_x(E + 2)
            sp.wait_ge(combined, E)
            sp.dma_start(ebuf[:, 0, :], fc).then_inc(fc_in, 16)
            sp.dma_start(ebuf[:, 1, :], proj).then_inc(fc_in, 16)
            sp.wait_ge(s_mm, 2 * T)
            sp.dma_start(lnwt[0:R], lnw).then_inc(lnw_in, 16)
            with sp.Fori(0, T - 1) as t:
                sp.wait_ge(done, t + 1)
                sp.dma_start(out[bass.ds(t * R, R), :], h[0:R, t, :]).then_inc(stored, 16)
            sp.wait_ge(done, T)
            sp.dma_start(out[B * S - (R - LAST_SKIP):B * S, :], h[LAST_SKIP:R, T - 1, :]).then_inc(stored, 16)
            sp.wait_ge(stored, 16 * T)

        @block.gpsimd
        def _(gp):
            gp.memset(half[:], -0.5).then_inc(init, 1)
            gp.memset(ones[:], 1.0).then_inc(init, 1)
            gp.memset(q_exp[:], 0.0).then_inc(init, 1)
            gp.memset(v0[:], 1.0).then_inc(init, 1)
            gp.memset(v1[:], 1.0).then_inc(init, 1)

            def split_x(t):
                gp.wait_ge(x_in, 16 * (t + 1))
                since(gp, patch_mm, t)
                stand(gp, gp_passed)
                gp.tensor_copy(xs[:, 0, :], x_raw[:]).then_inc(x_split, 1)
                gp.wait_ge(x_split, 2 * t + 1)
                gp.tensor_tensor(xs[:, 1, :], x_raw[:], xs[:, 0, :].bitcast(F32), ALU.subtract).then_inc(x_split, 1)

            def rstd(n, t, sem=None):
                gp.wait_ge(n["stat"], 3 * t + 3)
                gp.tensor_tensor(n["at"][0:R, 9:10], n["at"][0:R, 8:9], half[0:R], ALU.pow).then_inc(n["rstd"], 1)

            def a_step(t, split=True):
                rstd(nA, t)
                if split:
                    split_x(t + 1)
                gp.wait_ge(roped_parts, 3 * t + 3)
                since(gp, qkT_mm, t)
                gp.tensor_tensor(rq[0:R], rc[0:R], rs[0:R], ALU.add).then_inc(roped, 1)

            split_x(0)
            a_step(0)
            gp.wait_ge(wc_in, 16)
            gp.wait_ge(prep, 5)
            def a_step_wc(t):
                a_step(t)
                part = bass.ds((t - 1) * CHUNK, CHUNK)
                gp.tensor_copy(wc[:, 0, part], raw[:, part]).then_inc(wc_split, 1)
                gp.wait_ge(wc_split, 2 * t - 1)
                gp.tensor_tensor(wc[:, 1, part], raw[:, part], wc[:, 0, part].bitcast(F32), ALU.subtract).then_inc(wc_split, 1)

            a_step_wc(1)
            with gp.Fori(2, E + 1) as t:
                a_step_wc(t)
            a_step(E + 1)
            a_step(E + 2, False)

            def c1_add(t, experts):
                for e in experts:
                    gp.wait_ge(moe_scaled, E * t + e + 1)
                    since(gp, moe_acc, E * t + e)
                    if e == 0:
                        gp.wait_ge(n1["normed"], t + 1)
                    stand(gp, gp_passed)
                    gp.tensor_tensor(h[0:R, t, :], h[0:R, t, :], scaled[0:R, e % 4, :], ALU.add).then_inc(moe_acc, 1)

            def c2_keep(t):
                gp.wait_ge(n2["normed"], t + 1)
                stand(gp, gp_passed)
                gp.tensor_tensor(x1b[0:R, t, :], x1[0:R], row[0:R, BF:BF + D], ALU.add).then_inc(x1_kept, 1)

            def c3_h(t):
                gp.wait_ge(n4["normed"], t + 1)
                gp.tensor_tensor(r2[0:R], r2[0:R], row[0:R, BR2:BR2 + D], ALU.add).then_inc(h_r2, 1)
                gp.wait_ge(h_r2, 2 * t + 1)
                stand(gp, gp_passed)
                gp.tensor_tensor(h[0:R, t, :], h[0:R, t, :], r2[0:R], ALU.add).then_inc(h_r2, 1)

            def c_step(i, first, last):
                on = [first <= k <= last for k in range(5)]
                if on[2]:
                    rstd(n2, i - 2)
                if on[0]:
                    rstd(n1, i)
                if on[2]:
                    rstd(n3, i - 2)
                    c2_keep(i - 2)
                if on[4]:
                    rstd(n4, i - 4)
                if on[1]:
                    c1_add(i - 1, range(0, 4))
                if on[4]:
                    c3_h(i - 4)
                if on[1]:
                    c1_add(i - 1, range(4, E))

            for i in range(5):
                c_step(i, 0, i)
            with gp.Fori(5, T) as i:
                c_step(i, 0, 4)
            for i in range(T, T + 4):
                c_step(i, i - T + 1, 4)

            def d2(t):
                gp.wait_ge(g_stat, 4 * t + 4)
                stand(gp, gp_passed)
                gp.tensor_tensor(grs[0:R, t, 1:2], grs[0:R, t, 0:1], half[0:R], ALU.pow).then_inc(g_rstd, 1)
                gp.wait_ge(nD["normed"], t + 1)
                stand(gp, gp_passed)
                gp.tensor_tensor(h[0:R, t, :], h[0:R, t, :], bw[0:R], ALU.add).then_inc(hb_ready, 1)

            gp.wait_ge(bw_ready, 1)

            def d_step(i, first, last):
                on = [first <= k <= last for k in range(3)]
                if on[0]:
                    rstd(nD, i)
                if on[1]:
                    d2(i - 1)

            for i in range(3):
                d_step(i, 0, i)
            with gp.Fori(3, T) as i:
                d_step(i, 0, 2)
            d_step(T, 1, 2)

        @block.scalar
        def _(act):
            for i, (a, b, s) in enumerate(((A_P, A_QKV, wp_in), (A_QKV, A_O, wqkv_in), (A_O, A_END, wo_in))):
                act.wait_ge(s, 16)
                act.activation(wa[:, 0, a:b], raw[:, a:b], ACT.Copy).then_inc(wa_hi, 1)

            def turn_hi(tp, xh, src, t, free=None):
                act.wait_ge(tp["mm"], t + 1)
                if free:
                    since(act, *free)
                act.activation(xh[:], src, ACT.Copy).then_inc(tp["hi"], 1)

            def two(x):
                return x.rearrange("p (c r) -> p c r", c=DC)

            def affine_hi(tp, aff, y, xh, src, g, b, t, free):
                act.wait_ge(tp["mm"], t + 1)
                since(act, tp["lo"], t)
                for c in range(DC):
                    act.activation(y[:, c, :], src[:, c, :], ACT.Identity, bias=vec[:, b + c:b + c + 1],
                                   scale=vec[:, g + c:g + c + 1]).then_inc(aff, 1)
                act.wait_ge(aff, 2 * t + 2)
                since(act, *free)
                act.activation(xh[:], y[:], ACT.Copy).then_inc(tp["hi"], 1)

            def a1_x(t):
                turn_hi(tA, xth[0], two(bk[0][:, 256:256 + 2 * R]), t, (qkv_mm, t))

            def a1_v(t):
                act.wait_ge(qkv_mm, t + 1)
                since(act, pv0_mm, t)
                act.activation(v0[0:R, :, 0:HD], bk[2][0:R, 0:D].rearrange("p (h d) -> p h d", h=H),
                               ACT.Copy).then_inc(v0_ready, 1)

            def a1_q(t):
                act.wait_ge(qkT_mm, t + 1)
                since(act, s_mm, t)
                for f in range(2):
                    act.activation(qd(f),
                                   bk[2][:, f * R:(f + 1) * R].rearrange("p (b s) -> p b s", b=G),
                                   ACT.Copy).then_inc(q_ready, 1)

            def qd(f):
                return q_exp[:, f, :, 0:S]

            def softmax_exp(n):
                act.wait_ge(shifted, 2 * n + 2)
                since(act, pt_mm, 4 * n)
                for b in range(G):
                    act.activation(p_exp[0:R, :, b * S:(b + 1) * S], sc[0:R], ACT.Exp,
                                   bias=cst[0:R, CB + b:CB + b + 1], scale=SCALE).then_inc(exps, 1)

            def pt_out(n, free, groups):
                for g in groups:
                    act.wait_ge(pt_mm, 4 * n + g + 1)
                    if g == 0:
                        since(act, *free)
                    act.activation(pt[0:R, 4 * g:4 * g + 4, :], tb[g % 2][0:R, 0:4 * R].rearrange("p (h r) -> p h r", h=4),
                                   ACT.Copy).then_inc(pt_odd if g % 2 else pt_even, 1)

            def a2_o(t):
                turn_hi(tO, xth[1], two(bk2(1)[:, 0:2 * R]), t, (wo_mm, t))

            def expert_hi(e):
                act.wait_ge(combined, e + 1)
                act.activation(we_h[:, :, e, :], bz[:].rearrange("p (m n) -> p m n", m=DC), ACT.Copy).then_inc(we_hi, 1)

            act.wait_ge(init, 5)
            act.wait_ge(cst_in, 16)
            act.wait_ge(vec_in, 16)
            a1_x(0)
            a1_v(0)
            a1_q(0)

            def a_step(t, expert):
                softmax_exp(t - 1)
                pt_out(t - 1, (pv0_mm, t - 1), (0, 2))
                a1_x(t)
                a1_v(t)
                a2_o(t - 1)
                if expert:
                    expert_hi(t - 1)
                a1_q(t)

            a_step(1, True)
            with act.Fori(2, E + 1) as t:
                a_step(t, True)
            a_step(E + 1, False)
            a_step(E + 2, False)
            softmax_exp(T - 1)
            pt_out(T - 1, (pv0_mm, T - 1), (0, 2))
            a2_o(T - 1)

            def c1_x(t):
                turn_hi(t1, xth[0], two(bk[0][:, 0:2 * R]), t, (moe_mm, 4 * t))

            def c1_gate(t):
                act.wait_ge(gate_step, GS * t + 3)
                act.activation(gl[0:R, 3, :], gl[0:R, 2, :], ACT.Exp).then_inc(gate_exp, 1)

            def c2_x(t):
                affine_hi(t2, aff2, y2, xth[1], two(tb[0][:, 0:2 * R]), G1, B1, t, (v1_mm, t))

            def c2_rows(t):
                act.wait_ge(qk1_mm, t + 1)
                since(act, qkT1_mm, t)
                act.activation(qk_rows[0:R], tb[1][0:R, :], ACT.Copy).then_inc(qk1_out, 1)

            def c3_rows(t):
                act.wait_ge(wr1_mm, t + 1)
                since(act, r1T_mm, t)
                act.activation(r_rows[0:R], bz[0:R, :], ACT.Copy).then_inc(wr1_out, 1)

            def c2_q(t):
                act.wait_ge(qkT1_mm, t + 1)
                for f in range(2):
                    act.activation(qd(f), tb[0][:, f * R:(f + 1) * R].rearrange("p (b s) -> p b s", b=G),
                                   ACT.Identity, bias=vec[:, BQ + f:BQ + f + 1]).then_inc(q_ready, 1)

            def c2_pt(t):
                if isinstance(t, int) and t == 0:
                    pt_out(T, (pv0_mm, T), range(4))
                else:
                    pt_out(t + T, (pv1_mm, 6 * t), range(4))

            def c2_pv(t, groups):
                for g in groups:
                    h0, k = PV_GROUPS[g]
                    act.wait_ge(pv1_mm, 6 * t + g + 1)
                    if g == 0:
                        since(act, mix_step, MS * t)
                    act.activation(o1[0:R, h0:h0 + k, :],
                                   score[0:R, g % 2, 0:k * VE].rearrange("p (h d) -> p h d", h=k), ACT.Copy).then_inc(pv1_out, 1)

            def c2_mix(t):
                act.wait_ge(mix_step, MS * t + 5)
                act.activation(mx[0:R, 1, :], mx[0:R, 0, :], ACT.Exp).then_inc(mix_exp, 1)

            def c3_att(t):
                turn_hi(t3, xth[2], two(bz[:, 0:2 * R]), t, (wr1_mm, t))

            def c3_x(t):
                affine_hi(t4, aff4, y4, xth[2], two(bz[:, 0:2 * R]), G2, B2, t, (wf_mm, t + 1))

            def c3_relu(t):
                act.wait_ge(r1T_mm, t + 1)
                since(act, relu_lo, t)
                for j in range(4):
                    act.activation(r32[:, j * R:(j + 1) * R], bz[:, j * R:(j + 1) * R], ACT.Relu,
                                   bias=vec[:, BR1 + j:BR1 + j + 1]).then_inc(relu_32, 1)

            def c1_scale(t, pairs):
                for p in pairs:
                    act.wait_ge(moe_mm, 4 * t + p + 1)
                    act.wait_ge(gate_step, GS * t + GS)
                    for e in (2 * p, 2 * p + 1):
                        since(act, moe_acc, E * t + e - 3)
                        act.activation(scaled[0:R, e % 4, :], bk[1 + p % 2][0:R, (e % 2) * D:(e % 2 + 1) * D], ACT.Copy,
                                       scale=gl[0:R, 7, e:e + 1]).then_inc(moe_scaled, 1)

            def c_step(i, first, last):
                on = [first <= k <= last for k in range(5)]
                if on[3]:
                    c2_pt(i - 3)
                if on[1]:
                    c1_gate(i - 1)
                if on[3]:
                    c2_pv(i - 3, (0,))
                if on[4]:
                    c3_att(i - 4)
                if on[3]:
                    c2_pv(i - 3, (1, 2, 3))
                if on[2]:
                    c2_x(i - 2)
                if on[1]:
                    c1_scale(i - 1, (0, 1))
                if on[3]:
                    c2_pv(i - 3, (4, 5))
                if on[2]:
                    c2_rows(i - 2)
                if on[4]:
                    c3_x(i - 4)
                if on[2]:
                    c2_q(i - 2)
                if on[3]:
                    c2_mix(i - 3)
                if on[1]:
                    c1_scale(i - 1, (2,))
                if on[4]:
                    c3_rows(i - 4)
                    c3_relu(i - 4)
                if on[2]:
                    softmax_exp(i - 2 + T)
                if on[1]:
                    c1_scale(i - 1, (3,))
                if on[0]:
                    c1_x(i)

            for i in range(5):
                c_step(i, 0, i)
            with act.Fori(5, T) as i:
                c_step(i, 0, 4)
            for i in range(T, T + 4):
                c_step(i, i - T + 1, 4)

            def d1(t):
                turn_hi(tD, xth[0], two(bk[0][:, 0:2 * R]), t, (fc_mm, 2 * t))

            def d1_gelu(t):
                for q in range(2):
                    act.wait_ge(fc_mm, 2 * t + q + 1)
                    if q == 0:
                        since(act, gw_ready, t)
                    act.activation(gel[0:R, q * 512:(q + 1) * 512], bk[1 + q][0:R, :], ACT.Gelu).then_inc(gelu, 1)

            def d2_hi(t):
                for q in range(2):
                    act.wait_ge(gT_mm, 2 * t + q + 1)
                    if q == 0:
                        since(act, proj_mm, t)
                    act.activation(gth[:, 4 * q:4 * q + 4, :], score[:, q, 0:4 * R].rearrange("p (c r) -> p c r", c=4),
                                   ACT.Copy).then_inc(gT_hi, 1)

            def d_step(i, first, last):
                on = [first <= k <= last for k in range(3)]
                if on[2]:
                    d2_hi(i - 2)
                if on[1]:
                    d1_gelu(i - 1)
                if on[0]:
                    d1(i)

            for i in range(3):
                d_step(i, 0, i)
            with act.Fori(3, T) as i:
                d_step(i, 0, 2)
            for i in range(T, T + 2):
                d_step(i, i - T + 1, 2)

        @block.vector
        def _(dve):
            V = nc.vector

            def moments(*places):
                for n, src, dst, t, free in places:
                    stand(dve, dve_passed)
                    V.bn_stats(n["at"][0:R, 0:6], src).then_inc(n["stat"], 1)
                for n, src, dst, t, free in places:
                    dve.wait_ge(n["stat"], 3 * t + 1)
                    stand(dve, dve_passed)
                    V.bn_aggr(n["at"][0:R, 6:8], n["at"][0:R, 0:6]).then_inc(n["stat"], 1)
                for n, src, dst, t, free in places:
                    dve.wait_ge(n["stat"], 3 * t + 2)
                    V.tensor_scalar(n["at"][0:R, 8:9], n["at"][0:R, 7:8], EPS, None, ALU.add).then_inc(n["stat"], 1)

            def normed(*places):
                for n, src, dst, t, free in places:
                    dve.wait_ge(n["rstd"], t + 1)
                    since(dve, *free)
                    V.tensor_scalar(dst, src, n["at"][0:R, 6:7], n["at"][0:R, 9:10], ALU.subtract, ALU.mult).then_inc(n["normed"], 1)

            def norms(*places):
                moments(*places)
                normed(*places)

            def two(x):
                return x.rearrange("p (c r) -> p c r", c=DC)

            def turn_lo(tp, xh, xl, src, t):
                dve.wait_ge(tp["hi"], t + 1)
                V.tensor_tensor(xl[:], src, xh[:].bitcast(F32), ALU.subtract).then_inc(tp["lo"], 1)

            def affine_lo(tp, y, xh, xl, t):
                dve.wait_ge(tp["hi"], t + 1)
                V.tensor_tensor(xl[:], y[:], xh[:].bitcast(F32), ALU.subtract).then_inc(tp["lo"], 1)

            dve.wait_ge(init, 5)
            dve.wait_ge(row_in, 16)
            V.tensor_tensor(row[0:R, TOK:TOK + D], row[0:R, TOK:TOK + D], row[0:R, POS:POS + D], ALU.add).then_inc(table, 1)
            for i, (a, b) in enumerate(((A_P, A_QKV), (A_QKV, A_O), (A_O, A_END))):
                dve.wait_ge(wa_hi, i + 1)
                V.tensor_tensor(wa[:, 1, a:b], raw[:, a:b], wa[:, 0, a:b].bitcast(F32), ALU.subtract).then_inc(wa_lo, 1)
            dve.wait_ge(cst_in, 16)
            V.tensor_copy(idb[:], ident).then_inc(table, 1)
            V.tensor_copy(cmask[:], cst[:, CM:CW]).then_inc(table, 1)

            def a1_embed(t):
                dve.wait_ge(patch_mm, t + 1)
                V.tensor_tensor(h[0:R, t, :], bk[0][0:R, 0:D], row[0:R, TOK:TOK + D], ALU.add).then_inc(embedded, 1)
                dve.wait_ge(embedded, t + 1)
                norms((nA, h[0:R, t, :], xn[0:R], t, (tA["mm"], t)))

            def a1_x(t):
                turn_lo(tA, xth[0], xtl[0], two(bk[0][:, 256:256 + 2 * R]), t)

            def a1_rope(t):
                dve.wait_ge(qkv_mm, t + 1)
                since(dve, roped, t)
                qk = bk[1][0:R, :].rearrange("p (h d) -> p h d", d=HD)
                cos = cst[0:R, CC:CC + HD].unsqueeze(1).broadcast_to([R, 2 * H, HD])
                V.tensor_tensor(rc[0:R].rearrange("p (h d) -> p h d", d=HD), qk, cos, ALU.mult).then_inc(roped_parts, 1)
                for i in range(2):
                    a, b = i * HD // 2, (1 - i) * HD // 2
                    sin = cst[0:R, CS + a:CS + a + HD // 2].unsqueeze(1).broadcast_to([R, 2 * H, HD // 2])
                    V.tensor_tensor(rs[0:R].rearrange("p (h d) -> p h d", d=HD)[:, :, a:a + HD // 2],
                                    qk[:, :, b:b + HD // 2], sin, ALU.mult).then_inc(roped_parts, 1)

            def a1_k(t):
                dve.wait_ge(qkT_mm, t + 1)
                since(dve, s_mm, t)
                for f in range(2):
                    kT = bk[1][:, f * R:(1 + f) * R].unsqueeze(1).broadcast_to([P, HF, R])
                    V.tensor_tensor(k_exp[:, f], kT, hmask, ALU.mult).then_inc(k_ready, 1)

            def softmax_shift(n):
                dve.wait_ge(s_mm, n + 1)
                s = score[0:R, :, 0:HF * S].rearrange("p f (h j) -> p f h j", j=S)
                V.tensor_reduce(smax[0:R].rearrange("p (f h) -> p f h", f=2), s, AX, ALU.max).then_inc(s_max, 1)
                dve.wait_ge(s_max, n + 1)
                since(dve, exps, 3 * n)
                for f in range(2):
                    V.tensor_tensor(sc[0:R, f * HF:(f + 1) * HF, :], s[:, f],
                                    smax[0:R, f * HF:(f + 1) * HF].unsqueeze(2).broadcast_to([R, HF, S]),
                                    ALU.subtract).then_inc(shifted, 1)

            def pt_out(n, free):
                for g in (1, 3):
                    dve.wait_ge(pt_mm, 4 * n + g + 1)
                    if g == 1:
                        since(dve, *free)
                    V.tensor_copy(pt[0:R, 4 * g:4 * g + 4, :],
                                  tb[1][0:R, 0:4 * R].rearrange("p (h r) -> p h r", h=4)).then_inc(pt_odd, 1)

            def a2_o(t):
                dve.wait_ge(pv0_mm, t + 1)
                o = score[0:R, 0, 0:H * (HD + 1)].rearrange("p (h d) -> p h d", h=H)
                V.reciprocal(rinv0[0:R], o[:, :, HD]).then_inc(rinv0_ready, 1)
                dve.wait_ge(rinv0_ready, t + 1)
                since(dve, tO["mm"], t)
                V.tensor_tensor(att[0:R].rearrange("p (h d) -> p h d", h=H), o[:, :, 0:HD],
                                rinv0[0:R].unsqueeze(2).broadcast_to([R, H, HD]), ALU.mult).then_inc(o_ready, 1)

            def a2_lo(t):
                turn_lo(tO, xth[1], xtl[1], two(bk2(1)[:, 0:2 * R]), t)

            def a2_res(t):
                dve.wait_ge(wo_mm, t + 1)
                V.tensor_tensor(h[0:R, t, :], bk2(1)[0:R, 256:512], h[0:R, t, :], ALU.add).then_inc(res0, 1)

            def expert_lo(e):
                dve.wait_ge(we_hi, e + 1)
                V.tensor_tensor(we_l[:, :, e, :], bz[:].rearrange("p (m n) -> p m n", m=DC),
                                we_h[:, :, e, :].bitcast(F32), ALU.subtract).then_inc(we_lo, 1)

            a1_embed(0)
            a1_x(0)
            a1_rope(0)
            a1_k(0)

            dve.wait_ge(wc_in, 16)
            dve.wait_ge(vec_in, 16)
            wv = raw[:, C_V:C_G].rearrange("p (c n) -> p c n", c=DC)
            tmp = p_exp[:].rearrange("p h r -> p (h r)")
            wso = row[:, WSO:WSO + HD].unsqueeze(1)
            for c in range(DC):
                V.tensor_tensor(tmp[:, c * VW:(c + 1) * VW].rearrange("p (r d) -> p r d", r=RK),
                                wv[:, c, 0:VW].rearrange("p (r d) -> p r d", r=RK), wso.broadcast_to([P, RK, HD]),
                                ALU.mult).then_inc(table, 1)
            V.tensor_tensor(tmp[:, 2 * VW:3 * VW].rearrange("p (r d) -> p r d", r=RK),
                            row[:, BV:BV + VW].rearrange("p (r d) -> p r d", r=RK), wso.broadcast_to([P, RK, HD]),
                            ALU.mult).then_inc(table, 1)
            dve.wait_ge(table, 6)
            V.tensor_reduce(wv[:, :, VW:VW + RK], tmp[:, 0:2 * VW].rearrange("p (c r d) -> p c r d", c=DC, r=RK),
                            AX, ALU.add).then_inc(prep, 1)
            V.tensor_reduce(vtab[:, VW:VW + RK], tmp[:, 2 * VW:3 * VW].rearrange("p (r d) -> p r d", r=RK),
                            AX, ALU.add).then_inc(prep, 1)
            V.tensor_copy(vtab[:, 0:VW], row[:, BV:BV + VW]).then_inc(prep, 1)
            bl = tmp[:, 3 * VW:3 * VW + 4]
            V.tensor_scalar(bl, cst[:, CK:CK + 4], vec[:, WSQ:WSQ + 1], float(QK) ** -0.5, ALU.mult, ALU.mult).then_inc(table, 1)
            dve.wait_ge(table, 7)
            for c in range(4):
                V.tensor_scalar(tmp[:, 3 * VW + 4 + 4 * c:3 * VW + 8 + 4 * c], bl, vec[:, BQV + c:BQV + c + 1], None,
                                ALU.mult).then_inc(table, 1)
            dve.wait_ge(prep_mm, 1)
            V.tensor_copy(wv[:, :, VW + RK:W2], bz[:, 0:2 * H].rearrange("p (c h) -> p c h", c=DC)).then_inc(prep, 1)
            V.tensor_scalar(cb[:], bz[:, 2 * H:3 * H], row[:, BS:BS + 1], None, ALU.add).then_inc(prep, 1)

            def a_step(t, expert):
                softmax_shift(t - 1)
                a1_embed(t)
                pt_out(t - 1, (pv0_mm, t - 1))
                a1_x(t)
                a2_o(t - 1)
                a1_rope(t)
                a2_lo(t - 1)
                if expert:
                    expert_lo(t - 1)
                a2_res(t - 1)
                a1_k(t)

            a_step(1, True)
            with dve.Fori(2, E + 1) as t:
                a_step(t, True)
            a_step(E + 1, False)
            a_step(E + 2, False)
            softmax_shift(T - 1)
            pt_out(T - 1, (pv0_mm, T - 1))
            a2_o(T - 1)
            a2_lo(T - 1)
            a2_res(T - 1)

            def place1(t):
                dve.wait_ge(res0, t + 1)
                return n1, h[0:R, t, :], xn[0:R], t, (t1["mm"], t) if not isinstance(t, int) or t else (tA["mm"], T)

            def place2(t):
                dve.wait_ge(moe_acc, E * t + E)
                return n2, h[0:R, t, :], x1[0:R], t, (x1_kept, t)

            def place3(t):
                dve.wait_ge(n2["normed"], t + 1)
                return n3, x1[0:R], x2[0:R], t, (t2["mm"], t)

            def place4(t):
                dve.wait_ge(wf_mm, t + 1)
                dve.wait_ge(x1_kept, t + 1)
                since(dve, h_r2, 2 * t)
                V.tensor_tensor(r2[0:R], bz[0:R, 256:512], x1b[0:R, t, :], ALU.add).then_inc(r2_ready, 1)
                dve.wait_ge(r2_ready, t + 1)
                return n4, r2[0:R], x3[0:R], t, (t4["mm"], t)

            def c1_x(t):
                turn_lo(t1, xth[0], xtl[0], two(bk[0][:, 0:2 * R]), t)

            def c2_v_move(t):
                dve.wait_ge(v1_ready, 2 * t + 2)
                since(dve, pv1_mm, 6 * t)
                V.tensor_copy(v1[0:R, 0:VE - 1], v1_next[0:R]).then_inc(v1_moved, 1)

            def gate(t, k):
                g = gl[0:R]
                mine = g[:, 0, :].unsqueeze(2).broadcast_to([R, E, E])
                other = g[:, 0, :].unsqueeze(1).broadcast_to([R, E, E])
                before = cst[0:R, CT:CT + E * E].rearrange("p (a b) -> p a b", a=E)
                if k == 0:
                    dve.wait_ge(gate_mm, t + 1)
                    since(dve, moe_scaled, E * t)
                else:
                    dve.wait_ge(gate_step, GS * t + k)
                if k == 0:
                    ins = V.tensor_copy(g[:, 0, :], bk[0][0:R, 256:256 + E])
                elif k == 1:
                    ins = V.tensor_reduce(g[:, 1, 0:1], g[:, 0, :], AX, ALU.max)
                elif k == 2:
                    ins = V.tensor_scalar(g[:, 2, :], g[:, 0, :], g[:, 1, 0:1], None, ALU.subtract)
                elif k == 3:
                    ins = V.tensor_tensor(g8[0:R, 0], other, mine, ALU.is_gt)
                elif k == 4:
                    ins = V.tensor_tensor(g8[0:R, 1], other, mine, ALU.is_equal)
                elif k == 5:
                    ins = V.tensor_tensor(g8[0:R, 1], g8[0:R, 1], before, ALU.mult)
                elif k == 6:
                    ins = V.tensor_tensor(g8[0:R, 0], g8[0:R, 0], g8[0:R, 1], ALU.add)
                elif k == 7:
                    ins = V.tensor_reduce(g[:, 4, :], g8[0:R, 0], AX, ALU.add)
                elif k == 8:
                    dve.wait_ge(gate_exp, t + 1)
                    ins = V.scalar_tensor_tensor(g[:, 5, :], g[:, 4, :], 1.5, g[:, 3, :], ALU.is_lt, ALU.mult)
                elif k == 9:
                    ins = V.tensor_reduce(g[:, 6, 0:1], g[:, 5, :], AX, ALU.add)
                elif k == 10:
                    ins = V.reciprocal(g[:, 6, 1:2], g[:, 6, 0:1])
                else:
                    ins = V.tensor_scalar(g[:, 7, :], g[:, 5, :], g[:, 6, 1:2], None, ALU.mult)
                ins.then_inc(gate_step, 1)

            def c2_x(t):
                affine_lo(t2, y2, xth[1], xtl[1], t)

            def c2_k(t, halves):
                dve.wait_ge(qkT1_mm, t + 1)
                for f in halves:
                    kT = tb[1][:, f * R:(1 + f) * R].unsqueeze(1).broadcast_to([P, HF, R])
                    V.scalar_tensor_tensor(k_exp[:, f], kT, vec[:, BK + f:BK + f + 1], hmask,
                                           ALU.add, ALU.mult).then_inc(k_ready, 1)

            def c2_v(t):
                dve.wait_ge(v1_mm, t + 1)
                since(dve, v1_moved, t)
                V.tensor_tensor(v1_next[0:R], tb[0][0:R, 2 * R:2 * R + VE - 1], vtab[0:R], ALU.add).then_inc(v1_ready, 1)
                V.tensor_tensor(qvs[0:R, t, :], tb[0][0:R, 2 * R + VE - 1:2 * R + W2], cb[0:R], ALU.add).then_inc(v1_ready, 1)

            def mix(t, k):

                def over(x):
                    return x.unsqueeze(2).broadcast_to([R, H, RK])

                c = mx[0:R, 0].rearrange("p (h r) -> p h r", h=H)
                ex = mx[0:R, 1].rearrange("p (h r) -> p h r", h=H)
                w = mx[0:R, 2].rearrange("p (h r) -> p h r", h=H)
                o = o1[0:R, :, 0:VW].rearrange("p h (r d) -> p h r d", r=RK)
                rden, top, rsum = (mr[0:R, i] for i in range(3))
                if k == 0:
                    dve.wait_ge(pv1_out, 6 * t + 6)
                else:
                    dve.wait_ge(mix_step, MS * t + k)
                if k == 0:
                    ins = V.reciprocal(rden, o1[0:R, :, VE - 1])
                elif k == 1:
                    ins = V.tensor_tensor(c, o1[0:R, :, VW:VW + RK], over(rden), ALU.mult)
                elif k == 2:
                    dve.wait_ge(v1_ready, 2 * t + 2)
                    ins = V.tensor_tensor(c, c, over(qvs[0:R, t, :]), ALU.add)
                elif k == 3:
                    ins = V.tensor_reduce(top, c, AX, ALU.max)
                elif k == 4:
                    ins = V.tensor_tensor(c, c, over(top), ALU.subtract)
                elif k == 5:
                    dve.wait_ge(mix_exp, t + 1)
                    ins = V.tensor_reduce(top, ex, AX, ALU.add)
                elif k == 6:
                    ins = V.reciprocal(rsum, top)
                elif k == 7:
                    ins = V.tensor_tensor(rsum, rsum, rden, ALU.mult)
                elif k == 8:
                    ins = V.tensor_tensor(w, ex, over(rsum), ALU.mult)
                elif k == 9:
                    ins = V.tensor_tensor(o, o, w.unsqueeze(3).broadcast_to([R, H, RK, HD]), ALU.mult)
                else:
                    since(dve, t3["mm"], t)
                    if isinstance(t, int) and t == 0:
                        dve.wait_ge(tO["mm"], T)
                    ins = V.tensor_reduce(att[0:R].rearrange("p (h d) -> p h d", h=H), o.rearrange("p h r d -> p h d r"),
                                          AX, ALU.add)
                ins.then_inc(mix_step, 1)

            def c3_att(t):
                turn_lo(t3, xth[2], xtl[2], two(bz[:, 0:2 * R]), t)

            def c3_x(t):
                affine_lo(t4, y4, xth[2], xtl[2], t)

            def c3_relu(t):
                dve.wait_ge(relu_32, 4 * t + 4)
                since(dve, wr2_mm, t)
                V.tensor_copy(rh[:], r32.rearrange("p (j r) -> p j r", j=4)).then_inc(relu_hi, 1)
                dve.wait_ge(relu_hi, t + 1)
                V.tensor_tensor(rl[:], r32.rearrange("p (j r) -> p j r", j=4), rh[:].bitcast(F32), ALU.subtract).then_inc(relu_lo, 1)

            def c3_res(t):
                dve.wait_ge(wr2_mm, t + 1)
                dve.wait_ge(h_r2, 2 * t + 2)
                V.tensor_tensor(h[0:R, t, :], bz[0:R, 0:D], h[0:R, t, :], ALU.add).then_inc(res1, 1)

            def c_step(i, first, last):
                on = [first <= k <= last for k in range(5)]
                ones_two = [*([place2(i - 2)] if on[2] else []), *([place1(i)] if on[0] else [])]
                moments(*ones_two)
                if on[1]:
                    for k in range(3):
                        gate(i - 1, k)
                if on[4]:
                    c3_att(i - 4)
                normed(*ones_two)
                if on[2]:
                    three = place3(i - 2)
                    moments(three)
                if on[1]:
                    for k in range(3, 8):
                        gate(i - 1, k)
                if on[2]:
                    normed(three)
                if on[1]:
                    for k in range(8, GS):
                        gate(i - 1, k)
                if on[4]:
                    norms(place4(i - 4))
                if on[2]:
                    c2_x(i - 2)
                    c2_v(i - 2)
                if on[4]:
                    c3_x(i - 4)
                if on[2]:
                    c2_k(i - 2, (0, 1))
                if on[3]:
                    for k in range(MS - 2):
                        mix(i - 3, k)
                if on[2]:
                    c2_v_move(i - 2)
                    softmax_shift(i - 2 + T)
                if on[4]:
                    c3_relu(i - 4)
                if on[3]:
                    mix(i - 3, MS - 2)
                if on[0]:
                    c1_x(i)
                if on[3]:
                    mix(i - 3, MS - 1)
                if on[4]:
                    c3_res(i - 4)

            c_step(0, 0, 0)

            dve.wait_ge(fc_in, 32)
            for i in range(2):
                V.tensor_reduce(th[:, i:i + 1], ebuf[:, i, :], AX, ALU.add, apply_absolute_value=True).then_inc(tern, 1)
            dve.wait_ge(tern_mm, 1)
            V.tensor_scalar(th[:, 2:4], tb[0][:, 0:2], 0.5 / (D * HID), 0.5e-6, ALU.mult, ALU.add).then_inc(tern, 1)
            dve.wait_ge(tern, 3)
            V.tensor_scalar(th[:, 4:6], th[:, 2:4], -1.0, None, ALU.mult).then_inc(tern, 1)
            dve.wait_ge(tern, 4)
            dve.wait_ge(wo_mm, T)
            for i in range(2):
                V.tensor_scalar(wa[:, i, 0:HC * D], ebuf[:, i, :], th[:, 4 + i:5 + i], None, ALU.is_lt).then_inc(tern, 1)
            dve.wait_ge(tern, 6)
            for i in range(2):
                V.scalar_tensor_tensor(wa[:, i, 0:HC * D], ebuf[:, i, :], th[:, 2 + i:3 + i],
                                       wa[:, i, 0:HC * D].bitcast(F32), ALU.is_gt, ALU.subtract).then_inc(tern, 1)

            for i in range(1, 5):
                c_step(i, 0, i)
            with dve.Fori(5, T) as i:
                c_step(i, 0, 4)
            for i in range(T, T + 4):
                c_step(i, i - T + 1, 4)

            def d1_norm(t):
                dve.wait_ge(res1, t + 1)
                norms((nD, h[0:R, t, :], xn[0:R], t, (tD["mm"], t) if not isinstance(t, int) or t else (t1["mm"], T)))

            def d1_x(t):
                turn_lo(tD, xth[0], xtl[0], two(bk[0][:, 0:2 * R]), t)

            def d2_norm(t):
                st = mx[0:R, 0, 0:12]
                for q in range(2):
                    dve.wait_ge(gelu, 2 * t + q + 1)
                    V.bn_stats(st[:, 6 * q:6 * q + 6], gel[0:R, q * 512:(q + 1) * 512]).then_inc(g_stat, 1)
                dve.wait_ge(g_stat, 4 * t + 2)
                stand(dve, dve_passed)
                V.bn_aggr(mr[0:R, 0, 0:2], st).then_inc(g_stat, 1)
                dve.wait_ge(g_stat, 4 * t + 3)
                V.tensor_scalar(grs[0:R, t, 0:1], mr[0:R, 0, 1:2], EPS, None, ALU.add).then_inc(g_stat, 1)
                since(dve, gT_mm, 2 * t)
                V.scalar_tensor_tensor(gw[0:R], gel[0:R], mr[0:R, 0, 0:1], lnwt[0:R], ALU.subtract, ALU.mult).then_inc(gw_ready, 1)

            def d2_lo(t):
                for q in range(2):
                    dve.wait_ge(gT_hi, 2 * t + q + 1)
                    V.tensor_tensor(gtl[:, 4 * q:4 * q + 4, :], score[:, q, 0:4 * R].rearrange("p (c r) -> p c r", c=4),
                                    gth[:, 4 * q:4 * q + 4, :].bitcast(F32), ALU.subtract).then_inc(gT_lo, 1)

            def d2_out(t):
                dve.wait_ge(proj_mm, t + 1)
                dve.wait_ge(hb_ready, t + 1)
                dve.wait_ge(g_rstd, t + 1)
                V.scalar_tensor_tensor(h[0:R, t, :], tb[0][0:R, 0:D], grs[0:R, t, 1:2], h[0:R, t, :],
                                       ALU.mult, ALU.add).then_inc(done, 1)

            dve.wait_ge(pv1_mm, 6 * T)
            V.tensor_copy(pt[:, 0:HC, :], vec[:, LNB:LNB + HC].unsqueeze(2).broadcast_to([P, HC, R])).then_inc(tern, 1)
            dve.wait_ge(tern_mm, 2)
            V.tensor_copy(bw[0:R], tb[1][0:R, 0:D]).then_inc(bw_ready, 1)
            dve.wait_ge(lnw_in, 16)

            def d_step(i, first, last):
                on = [first <= k <= last for k in range(3)]
                if on[2]:
                    d2_lo(i - 2)
                if on[0]:
                    d1_norm(i)
                if on[1]:
                    d2_norm(i - 1)
                if on[2]:
                    d2_out(i - 2)
                if on[0]:
                    d1_x(i)

            for i in range(3):
                d_step(i, 0, i)
            with dve.Fori(3, T) as i:
                d_step(i, 0, 2)
            for i in range(T, T + 2):
                d_step(i, i - T + 1, 2)

        @block.tensor
        def _(pe):
            def mm3(dst, lh, ll, rh_, rl_, first, last):
                pe.matmul(dst, lh, rh_, start=first, stop=False)
                pe.matmul(dst, lh, rl_, start=False, stop=False)
                return pe.matmul(dst, ll, rh_, start=False, stop=last)

            def product(dst, xh, xl, w, at, width, cols):
                a, b = cols
                for c in range(DC):
                    o = at + c * width
                    last = mm3(dst, xh[:, c, :], xl[:, c, :], w[:, 0, o + a:o + b], w[:, 1, o + a:o + b], c == 0, c == DC - 1)
                return last

            def turned(dst, x):
                for c in range(DC):
                    last = pe.transpose(dst[:, c * R:(c + 1) * R], x[0:R, c * P:(c + 1) * P], cst[0:R, CI:CI + R])
                return last

            def turn(tp, dst, x, ready, t):
                pe.wait_ge(ready, t + 1)
                turned(dst, x).then_inc(tp["mm"], 1)

            def a1_patch(t):
                pe.wait_ge(x_split, 2 * t + 2)
                since(pe, tA["lo"], t)
                for c in range(NP):
                    last = mm3(bk[0][0:R, 0:D], xs[:, 0, c * R:(c + 1) * R], xs[:, 1, c * R:(c + 1) * R],
                               wa[:, 0, A_P + c * D:A_P + (c + 1) * D], wa[:, 1, A_P + c * D:A_P + (c + 1) * D],
                               c == 0, c == NP - 1)
                last.then_inc(patch_mm, 1)

            def a1_x(t):
                turn(tA, bk[0][:, 256:256 + 2 * R], xn, nA["normed"], t)

            def a1_qkv(t):
                pe.wait_ge(tA["lo"], t + 1)
                since(pe, k_ready, 2 * t)
                since(pe, q_ready, 2 * t)
                product(bk[1][0:R, :], xth[0], xtl[0], wa, A_QKV, 3 * D, (0, 2 * D))
                product(bk[2][0:R, 0:D], xth[0], xtl[0], wa, A_QKV, 3 * D, (2 * D, 3 * D)).then_inc(qkv_mm, 1)

            def a1_qkT(t):
                pe.wait_ge(roped, t + 1)
                pe.wait_ge(v0_ready, t + 1)
                turned(bk[2][:, 0:2 * R], rq[:, 0:D])
                turned(bk[1][:, 0:2 * R], rq[:, D:2 * D]).then_inc(qkT_mm, 1)

            def scores(n, causal):
                pe.wait_ge(q_ready, 2 * n + 2)
                pe.wait_ge(k_ready, 2 * n + 2)
                for f in range(2):
                    dst = score[0:R, f, 0:HF * S]
                    if causal:
                        pe.matmul(dst, idb[0:R, 0:R], cmask[0:R], start=True, stop=False)
                    for b in range(G):
                        last = pe.matmul(dst, q_exp[:, f].rearrange("p b x -> p (b x)")[:, b * R:(b + 1) * R],
                                         k_exp[:, f, :, b * S:(b + 1) * S], start=(not causal and b == 0), stop=(b == G - 1))
                last.then_inc(s_mm, 1)

            def turn_p(n):
                pe.wait_ge(exps, 3 * n + 3)
                for g in range(4):
                    if g % 2 == 0:
                        since(pe, pt_even, 2 * n + g // 2)
                    else:
                        since(pe, pt_odd, 2 * n + g // 2)
                    for i in range(4):
                        last = pe.transpose(tb[g % 2][0:R, i * R:(i + 1) * R], p_exp[0:R, 4 * g + i, :], cst[0:R, CI:CI + R])
                    last.then_inc(pt_mm, 1)

            def a2_pv(t):
                pe.wait_ge(pt_even, 2 * t + 2)
                pe.wait_ge(pt_odd, 2 * t + 2)
                pe.wait_ge(v0_ready, t + 1)
                for i in range(H):
                    last = pe.matmul(score[0:R, 0, i * (HD + 1):(i + 1) * (HD + 1)], pt[0:R, i, :], v0[0:R, i, :],
                                     start=True, stop=True)
                last.then_inc(pv0_mm, 1)

            def a2_o(t):
                turn(tO, bk2(1)[:, 0:2 * R], att, o_ready, t)

            def a2_wo(t):
                pe.wait_ge(tO["lo"], t + 1)
                product(bk2(1)[0:R, 256:512], xth[1], xtl[1], wa, A_O, D, (0, D)).then_inc(wo_mm, 1)

            def combine(e, m):
                if m == 0:
                    pe.wait_ge(expert_in, 32 * e + 32)
                    since(pe, we_lo, e)
                for c in range(HC):
                    last = pe.matmul(bz[:, m * D:(m + 1) * D], ebuf[:, 0, c * D + m * P:c * D + (m + 1) * P],
                                     ebuf[:, 1, c * D:(c + 1) * D], start=(c == 0), stop=(c == HC - 1))
                if m == DC - 1:
                    last.then_inc(combined, 1)

            pe.wait_ge(wa_lo, 3)
            pe.wait_ge(cst_in, 16)
            pe.wait_ge(table, 3)
            pe.wait_ge(init, 5)
            a1_patch(0)
            a1_x(0)
            a1_qkv(0)
            a1_qkT(0)
            pe.wait_ge(wqv_in, 16)
            pe.wait_ge(table, 11)
            tmp = p_exp[:].rearrange("p h r -> p (h r)")
            for c in range(4):
                for m in range(DC):
                    pe.matmul(bz[:, m * H + 4 * c:m * H + 4 * c + 4], ptf[:, c * D + m * P:c * D + (m + 1) * P],
                              tmp[:, 3 * VW:3 * VW + 4], start=True, stop=True)
                last = pe.matmul(bz[:, 2 * H + 4 * c:2 * H + 4 * c + 4], ones[:],
                                 tmp[:, 3 * VW + 4 + 4 * c:3 * VW + 8 + 4 * c], start=True, stop=True)
            last.then_inc(prep_mm, 1)
            pe.wait_ge(prep, 5)

            def a_step(t, expert):
                scores(t - 1, True)
                a1_patch(t)
                if expert:
                    combine(t - 1, 0)
                turn_p(t - 1)
                a1_x(t)
                a2_pv(t - 1)
                a1_qkv(t)
                a2_o(t - 1)
                if expert:
                    combine(t - 1, 1)
                a2_wo(t - 1)
                a1_qkT(t)

            a_step(1, True)
            with pe.Fori(2, E + 1) as t:
                a_step(t, True)
            a_step(E + 1, False)
            a_step(E + 2, False)
            scores(T - 1, True)
            turn_p(T - 1)
            a2_pv(T - 1)
            a2_o(T - 1)
            a2_wo(T - 1)

            def c1_x(t):
                turn(t1, bk[0][:, 0:2 * R], xn, n1["normed"], t)

            def c1_gate(t):
                pe.wait_ge(t1["lo"], t + 1)
                product(bk[0][0:R, 256:256 + E], xth[0], xtl[0], wc, C_G, E, (0, E)).then_inc(gate_mm, 1)

            def c1_moe(t, pairs):
                for p in pairs:
                    since(pe, moe_scaled, E * t + 2 * (p - 1))
                    for c in range(DC):
                        last = mm3(bk[1 + p % 2][0:R, :], xth[0][:, c, :], xtl[0][:, c, :],
                                   we_h[:, c, 2 * p:2 * p + 2, :].rearrange("p e d -> p (e d)"),
                                   we_l[:, c, 2 * p:2 * p + 2, :].rearrange("p e d -> p (e d)"), c == 0, c == DC - 1)
                    last.then_inc(moe_mm, 1)

            def c2_x(t):
                since(pe, pt_even, 2 * (t + T))
                since(pe, pt_odd, 2 * (t + T))
                turn(t2, tb[0][:, 0:2 * R], x2, n3["normed"], t)

            def c2_qkv(t):
                pe.wait_ge(t2["lo"], t + 1)
                product(tb[1][0:R, :], xth[1], xtl[1], wc, C_QK, 2 * D, (0, 2 * D)).then_inc(qk1_mm, 1)
                product(tb[0][0:R, 2 * R:2 * R + W2], xth[1], xtl[1], wc, C_V, W2, (0, W2)).then_inc(v1_mm, 1)

            def c2_qkT(t):
                pe.wait_ge(qk1_out, t + 1)
                pe.wait_ge(v1_ready, 2 * t + 2)
                turned(tb[0][:, 0:2 * R], qk_rows[:, 0:D])
                turned(tb[1][:, 0:2 * R], qk_rows[:, D:2 * D]).then_inc(qkT1_mm, 1)

            def c2_pv(t, groups):
                pe.wait_ge(pt_even, 2 * (t + T) + 2)
                pe.wait_ge(pt_odd, 2 * (t + T) + 2)
                pe.wait_ge(v1_moved, t + 1)
                for g in groups:
                    h0, k = PV_GROUPS[g]
                    if g >= 2:
                        pe.wait_ge(pv1_out, 6 * t + g - 1)
                    for i in range(k):
                        last = pe.matmul(score[0:R, g % 2, i * VE:(i + 1) * VE], pt[0:R, h0 + i, :], v1[0:R, :],
                                         start=True, stop=True)
                    last.then_inc(pv1_mm, 1)

            def c3_att(t):
                since(pe, res1, t)
                pe.wait_ge(mix_step, MS * t + MS)
                turned(bz[:, 0:2 * R], att).then_inc(t3["mm"], 1)

            def c3_wf(t):
                pe.wait_ge(t3["lo"], t + 1)
                product(bz[0:R, 256:512], xth[2], xtl[2], wc, C_F, D, (0, D)).then_inc(wf_mm, 1)

            def c3_x(t):
                turn(t4, bz[:, 0:2 * R], x3, n4["normed"], t)

            def c3_r1(t):
                pe.wait_ge(t4["lo"], t + 1)
                product(bz[0:R, :], xth[2], xtl[2], wc, C_R1, 2 * D, (0, 2 * D)).then_inc(wr1_mm, 1)

            def c3_r1T(t):
                pe.wait_ge(wr1_out, t + 1)
                turned(bz[:, 0:2 * R], r_rows[:, 0:D])
                turned(bz[:, 2 * R:4 * R], r_rows[:, D:2 * D]).then_inc(r1T_mm, 1)

            def c3_r2(t):
                pe.wait_ge(relu_lo, t + 1)
                for j in range(4):
                    o = C_R2 + j * D
                    last = mm3(bz[0:R, 0:D], rh[:, j, :], rl[:, j, :], wc[:, 0, o:o + D], wc[:, 1, o:o + D], j == 0, j == 3)
                last.then_inc(wr2_mm, 1)

            def c_step(i, first, last):
                on = [first <= k <= last for k in range(5)]
                if on[3]:
                    turn_p(i - 3 + T)
                if on[1]:
                    c1_gate(i - 1)
                if on[3]:
                    c2_pv(i - 3, (0, 1))
                if on[4]:
                    c3_att(i - 4)
                if on[1]:
                    c1_moe(i - 1, (0,))
                if on[3]:
                    c2_pv(i - 3, (2, 3))
                if on[4]:
                    c3_wf(i - 4)
                if on[2]:
                    c2_x(i - 2)
                if on[1]:
                    c1_moe(i - 1, (1,))
                if on[3]:
                    c2_pv(i - 3, (4, 5))
                if on[2]:
                    c2_qkv(i - 2)
                if on[4]:
                    c3_x(i - 4)
                if on[2]:
                    c2_qkT(i - 2)
                if on[1]:
                    c1_moe(i - 1, (2,))
                if on[4]:
                    c3_r1(i - 4)
                if on[2]:
                    scores(i - 2 + T, False)
                if on[4]:
                    c3_r1T(i - 4)
                if on[1]:
                    c1_moe(i - 1, (3,))
                if on[0]:
                    c1_x(i)
                if on[4]:
                    c3_r2(i - 4)

            pe.wait_ge(wc_split, 2 * E)
            c_step(0, 0, 0)
            pe.wait_ge(tern, 2)
            pe.wait_ge(pt_even, 2 * T)
            pe.matmul(tb[0][:, 0:2], ones[:], th[:, 0:2], start=True, stop=True).then_inc(tern_mm, 1)
            pe.wait_ge(tern, 3)
            for i in range(1, 5):
                c_step(i, 0, i)
            with pe.Fori(5, T) as i:
                c_step(i, 0, 4)
            for i in range(T, T + 4):
                c_step(i, i - T + 1, 4)

            pe.wait_ge(tern, 9)
            for c in range(HC):
                last = pe.matmul(tb[1][0:R, 0:D], pt[:, c, :], projt[:, c, :].bitcast(F32), start=(c == 0), stop=(c == HC - 1))
            last.then_inc(tern_mm, 1)

            def d1_x(t):
                turn(tD, bk[0][:, 0:2 * R], xn, nD["normed"], t)

            def d1_fc(t):
                pe.wait_ge(tD["lo"], t + 1)
                since(pe, gelu, 2 * t)
                for q in range(2):
                    for c in range(DC):
                        w = fct[:, c, q * 512:(q + 1) * 512]
                        pe.matmul(bk[1 + q][0:R, :], xth[0][:, c, :], w, start=(c == 0), stop=False)
                        last = pe.matmul(bk[1 + q][0:R, :], xtl[0][:, c, :], w, start=False, stop=(c == DC - 1))
                    last.then_inc(fc_mm, 1)

            def d2_turn(t):
                pe.wait_ge(gw_ready, t + 1)
                since(pe, gT_lo, 2 * t)
                for q in range(2):
                    for c in range(4):
                        k = 4 * q + c
                        last = pe.transpose(score[:, q, c * R:(c + 1) * R], gw[0:R, k * P:(k + 1) * P], cst[0:R, CI:CI + R])
                    last.then_inc(gT_mm, 1)

            def d2_proj(t):
                pe.wait_ge(gT_lo, 2 * t + 2)
                since(pe, done, t)
                for c in range(HC):
                    pe.matmul(tb[0][0:R, 0:D], gth[:, c, :], projt[:, c, :], start=(c == 0), stop=False)
                    last = pe.matmul(tb[0][0:R, 0:D], gtl[:, c, :], projt[:, c, :], start=False, stop=(c == HC - 1))
                last.then_inc(proj_mm, 1)

            def d_step(i, first, last):
                on = [first <= k <= last for k in range(3)]
                if on[2]:
                    d2_turn(i - 2)
                if on[1]:
                    d1_fc(i - 1)
                if on[2]:
                    d2_proj(i - 2)
                if on[0]:
                    d1_x(i)

            for i in range(3):
                d_step(i, 0, i)
            with pe.Fori(3, T) as i:
                d_step(i, 0, 2)
            for i in range(T, T + 2):
                d_step(i, i - T + 1, 2)


def lay_out(i):
    f = np.float32
    a = {k: np.asarray(v) for k, v in i.items()}
    n = IMG // PATCH

    def chunks(w, c):
        return w.reshape(c, P, -1).transpose(1, 0, 2).reshape(P, -1)

    def column(v, c):
        return v.reshape(c, P).T

    x = a["x"].reshape(B, CIN, n, PATCH, n, PATCH).transpose(1, 3, 5, 0, 2, 4).reshape(NP, P, B, n * n)
    xt = np.zeros((T, P, NP, G, S), f)
    for t in range(T):
        b0 = min(G * t, B - G)
        xt[t, :, :, :, 2:] = x[:, :, b0:b0 + G].transpose(1, 0, 2, 3)
    rows = np.zeros((P, RW), f)
    tok = np.concatenate([a["cls_tok"].reshape(1, D), a["L0_tok_cls_token"].reshape(1, D),
                          np.broadcast_to(a["L0_tok_b"], (S - 2, D))], 0)
    pos = np.concatenate([np.zeros((1, D), f), a["L0_tok_pos_embed"].reshape(S - 1, D)], 0)
    rows[:R, TOK:TOK + D] = np.tile(tok, (G, 1))
    rows[:R, POS:POS + D] = np.tile(pos, (G, 1))
    ws = a["L1_attn_Ws"].reshape(-1)
    for at, v in ((BV, a["L1_attn_bv"]), (BF, a["L1_attn_bf"]), (BR2, a["L1_attn_br2"]), (WSO, ws[QK:]), (BS, a["L1_attn_bs"])):
        rows[:, at:at + v.size] = v
    vectors = np.concatenate(
        [column(a["L1_attn_g1"], 2), column(a["L1_attn_b1"], 2), column(a["L1_attn_g2"], 2), column(a["L1_attn_b2"], 2),
         column(a["L1_attn_bq"], 2), column(a["L1_attn_bk"], 2), column(a["L1_attn_br1"], 4), column(a["L1_ffn_ln_b"], HC),
         column(a["L1_attn_bqv"], 4), np.tile(ws[:QK], 4)[:, None]], 1)
    w_a = np.concatenate(
        [chunks(a["L0_tok_W"].T, NP), chunks(np.concatenate([a["L0_attn_Wq"].T, a["L0_attn_Wk"].T, a["L0_attn_Wv"].T], 1), DC),
         chunks(a["L0_attn_Wo"].T, DC)], 1)
    wv = np.concatenate([a["L1_attn_Wv"].T, np.zeros((D, W2 - VW), f)], 1)
    w_c = np.concatenate(
        [chunks(np.concatenate([a["L1_attn_Wq"].T, a["L1_attn_Wk"].T], 1), DC), chunks(wv, DC), chunks(a["L0_ffn_w_gate"].T, DC),
         chunks(a["L1_attn_Wf"].T, DC), chunks(a["L1_attn_Wr1"].T, DC), chunks(a["L1_attn_Wr2"].T, 4)], 1)
    return {
        "x_tiles": xt.reshape(T, P, NP * R), "consts": constants(), "vectors": vectors, "rows": rows,
        "w_a": w_a, "w_c": w_c, "wqv": chunks(a["L1_attn_Wqv"], 4),
        "w_in": a["L0_ffn_w_in"].reshape(E, P, HC * D), "w_out": a["L0_ffn_w_out"].transpose(0, 2, 1).reshape(E, P, HC * D),
        "fc": chunks(a["L1_ffn_W_fc"].T, DC), "proj": chunks(a["L1_ffn_W_proj"].T, HC),
        "lnw": np.broadcast_to(a["L1_ffn_ln_w"], (R, HID)),
    }


def kernel(**inputs):
    import concourse.bacc as bacc
    from concourse.bass_utils import run_bass_kernel_spmd as run

    nc = bacc.Bacc("TRN2", target_bir_lowering=False, num_devices=1)
    arrays = {f"in_{k}": np.ascontiguousarray(v) for k, v in lay_out(inputs).items()}
    args = [nc.dram_tensor(k, v.shape, mybir.dt.from_np(v.dtype), kind="ExternalInput").ap() for k, v in arrays.items()]
    out = nc.dram_tensor("out_0", (B * S, D), F32, kind="ExternalOutput").ap()
    vit_tower(nc, *args, out)
    r = run(nc, [arrays], core_ids=[0])
    return r.results[0]["out_0"].reshape(B, S, D)
```
